# Optimizing a Trainium2 kernel written in Bass

```python
import numpy as np
import jax
import jax.numpy as jnp

def _softmax(x, axis=-1):
    return jax.nn.softmax(x, axis=axis)
def _gelu(x):
    return jax.nn.gelu(x, approximate=True)
def _silu(x):
    return jax.nn.silu(x)
def _sigmoid(x):
    return jax.nn.sigmoid(x)
def _layernorm(x, axis=-1, eps=1e-5):
    m = jnp.mean(x, axis=axis, keepdims=True)
    v = jnp.var(x, axis=axis, keepdims=True)
    return (x - m) / jnp.sqrt(v + eps)
def _scatter_add(tgt, idx, src, axis=0):
    return tgt.at[idx].add(src)
def _segment_sum(src, seg, n):
    return jax.ops.segment_sum(src, seg, n)

kernel_name = 'mk_conv_seq_d1_conv_nchw256_8f67ee'

def setup_inputs(seed: int = 0):
    np.random.seed(seed)
    _w = jnp.asarray
    def _rec_inputs():
        import jax
        import jax.numpy as jnp
        _gk = jax.random.key(seed)
        x = 7.22e-05 + 1 * jax.random.normal(jax.random.fold_in(_gk, 1), (32, 256, 32, 32), jnp.float32)
        return x
    x = _rec_inputs()
    def _L0_conv_setup():
        import jax, jax.numpy as jnp
        import numpy as np
        GROUPS = 8
        EPS = 1e-05

        def _group_norm(x, w, b):
            B, C, H, W = x.shape
            xr = x.reshape(B, GROUPS, C // GROUPS, H, W)
            mean = xr.mean(axis=(2, 3, 4), keepdims=True)
            var = xr.var(axis=(2, 3, 4), keepdims=True)
            h = (xr - mean) * jax.lax.rsqrt(var + EPS)
            h = h.reshape(B, C, H, W)
            return h * w[None, :, None, None] + b[None, :, None, None]
        key = jax.random.key(seed)
        ks = jax.random.split(key, 4)
        B, C, H, W = (32, 256, 32, 32)
        x = jax.random.normal(ks[0], (B, C, H, W), dtype=jnp.float32)
        norm_w = jnp.ones((C,), dtype=jnp.float32)
        norm_b = jnp.zeros((C,), dtype=jnp.float32)
        qkv_w = jax.random.normal(ks[1], (3 * C, C), dtype=jnp.float32) * (1.0 / np.sqrt(C))
        qkv_b = jnp.zeros((3 * C,), dtype=jnp.float32)
        proj_w = jax.random.normal(ks[2], (C, C), dtype=jnp.float32) * (1.0 / np.sqrt(C))
        proj_b = jnp.zeros((C,), dtype=jnp.float32)
        return {'x': x, 'norm_w': norm_w, 'norm_b': norm_b, 'qkv_w': qkv_w, 'qkv_b': qkv_b, 'proj_w': proj_w, 'proj_b': proj_b}
    _L0_conv_all = _L0_conv_setup()
    _L0_conv_in = {k: v for k, v in _L0_conv_all.items() if k in ('norm_w', 'norm_b', 'qkv_w', 'qkv_b', 'proj_w', 'proj_b', )}
    del _L0_conv_all

    return {
        "x": x,
        "L0_conv_norm_w": _L0_conv_in["norm_w"],
        "L0_conv_norm_b": _L0_conv_in["norm_b"],
        "L0_conv_qkv_w": _L0_conv_in["qkv_w"],
        "L0_conv_qkv_b": _L0_conv_in["qkv_b"],
        "L0_conv_proj_w": _L0_conv_in["proj_w"],
        "L0_conv_proj_b": _L0_conv_in["proj_b"],
    }

def reference(x, L0_conv_norm_w, L0_conv_norm_b, L0_conv_qkv_w, L0_conv_qkv_b, L0_conv_proj_w, L0_conv_proj_b):
    import jax
    import jax.numpy as jnp
    def _L0_conv_ref(x, norm_w, norm_b, qkv_w, qkv_b, proj_w, proj_b):
        import jax, jax.numpy as jnp
        import numpy as np
        GROUPS = 8
        EPS = 1e-05

        def _group_norm(x, w, b):
            B, C, H, W = x.shape
            xr = x.reshape(B, GROUPS, C // GROUPS, H, W)
            mean = xr.mean(axis=(2, 3, 4), keepdims=True)
            var = xr.var(axis=(2, 3, 4), keepdims=True)
            h = (xr - mean) * jax.lax.rsqrt(var + EPS)
            h = h.reshape(B, C, H, W)
            return h * w[None, :, None, None] + b[None, :, None, None]
        B, C, H, W = x.shape
        h = _group_norm(x, norm_w, norm_b)
        qkv = jnp.einsum('bchw,oc->bohw', h, qkv_w) + qkv_b[None, :, None, None]
        q, k, v = jnp.split(qkv, 3, axis=1)
        N = H * W
        q = q.reshape(B, C, N).transpose(0, 2, 1)
        k = k.reshape(B, C, N)
        v = v.reshape(B, C, N).transpose(0, 2, 1)
        scale = C ** (-0.5)
        attn = jax.nn.softmax(jnp.einsum('bqc,bck->bqk', q, k) * scale, axis=-1)
        h = jnp.einsum('bqk,bkc->bqc', attn, v)
        h = h.transpose(0, 2, 1).reshape(B, C, H, W)
        h = jnp.einsum('bchw,oc->bohw', h, proj_w) + proj_b[None, :, None, None]
        return x + h

    def _gn(v, G=32, eps=1e-5):
        B_, C_, H_, W_ = v.shape
        g = v.reshape(B_, G, C_ // G, H_, W_)
        m = jnp.mean(g, axis=(2, 3, 4), keepdims=True)
        s = jnp.var(g, axis=(2, 3, 4), keepdims=True)
        return ((g - m) / jnp.sqrt(s + eps)).reshape(v.shape)

    def _ln_c(v, eps=1e-6):
        m = jnp.mean(v, axis=1, keepdims=True)
        s = jnp.var(v, axis=1, keepdims=True)
        return (v - m) / jnp.sqrt(s + eps)

    def _ln_t(v, eps=1e-5):
        m = jnp.mean(v, axis=-1, keepdims=True)
        s = jnp.var(v, axis=-1, keepdims=True)
        return (v - m) / jnp.sqrt(s + eps)

    def _to_tokens(v):
        B_, C_, H_, W_ = v.shape
        return v.reshape(B_, C_, H_ * W_).transpose(0, 2, 1)
    def _from_tokens(t, like):
        B_, C_, H_, W_ = like.shape
        return t.transpose(0, 2, 1).reshape(B_, C_, H_, W_)

    x = _L0_conv_ref(x, L0_conv_norm_w, L0_conv_norm_b, L0_conv_qkv_w, L0_conv_qkv_b, L0_conv_proj_w, L0_conv_proj_b)
    return x


_drawn_inputs = setup_inputs


def setup_inputs(seed=0):
    import zlib

    import numpy as np

    out = dict(_drawn_inputs(seed))
    spreads = {'L0_conv_norm_w': (1.0, 0.2),
     'L0_conv_norm_b': (0.0, 0.1),
     'L0_conv_qkv_b': (0.0, 0.1),
     'L0_conv_proj_b': (0.0, 0.1)}
    factors = {}
    for name, (base, spread) in spreads.items():
        noise = np.random.default_rng([zlib.crc32(name.encode()), seed]).standard_normal(out[name].shape)
        drawn = base * np.exp(spread * noise) if base else spread * noise
        out[name] = jnp.asarray(drawn.astype(out[name].dtype))
    for name, factor in factors.items():
        out[name] = (out[name] * factor).astype(out[name].dtype)
    return out
```

```python
from contextlib import ExitStack

import concourse.bass as bass
from concourse import mybir


def attention_program(nc, x, norm_w, norm_b, qkv_w, qkv_b_cols, proj_w_t, proj_b_cols, out):
    f32, f16 = mybir.dt.float32, mybir.dt.float16
    ALU = mybir.AluOpType
    ACT = mybir.ActivationFunctionType
    AX = mybir.AxisListType

    P = 128
    B, C, HH, WW = x.shape
    N = HH * WW
    CK = C // P
    QT = N // P
    HALF_SLOTS = 2
    HALF = N // 2
    GROUP = C // 8
    EPS = 1e-5
    SCALE = float(C) ** -0.5
    TOP = 4.0
    VEC = 4096.0
    LN_P = 6.931471805599453
    VW = C + 1
    VP = VW + 1
    KPIECES = 2 * CK
    PIECES = KPIECES + QT
    GQ = N // HALF_SLOTS
    GT = GQ // P
    PAIRS = QT // 2
    BANKS = 4
    XRING = 4

    VALUES_BEFORE = {0: 0, 2: 3, 4: 5, 6: 7}
    VALUES_BEHIND = {0: 1, 1: 2, 3: 4, 5: 6}
    KEYS_BEFORE = {4: 1, 6: 3}
    KEYS_BEHIND = {3: 0, 5: 2}
    EXP_AT = {3: 0, 4: 1, 5: 2, 6: 3}
    LOW_AT = {4: 0, 5: 1, 6: 2, 7: 3}

    x_v = x.rearrange("b (c p) h w -> b p c (h w)", p=P)
    out_v = out.rearrange("b (c p) h w -> b p c (h w)", p=P)

    ctx = ExitStack()
    with ctx:
        def sb(name, shape, dt):
            return ctx.enter_context(nc.sbuf_tensor(name, shape, dt))

        def sem(name):
            return ctx.enter_context(nc.semaphore(name))

        ximg = sb("ximg", [P, XRING, CK, N], f32)
        norm32 = sb("norm32", [P, CK, N], f32)
        n_hi = sb("n_hi", [P, 2, CK, N], f16)
        n_lo = sb("n_lo", [P, 2, CK, N], f16)
        t_hi = sb("t_hi", [P, 2, CK, N], f16)
        t_lo = sb("t_lo", [P, 2, CK, N], f16)
        v_hi = sb("v_hi", [P, 2, QT, VP], f16)
        v_lo = sb("v_lo", [P, 2, QT, VP], f16)
        score = [sb(f"score{h}", [P, QT, GQ], f32) for h in range(2)]
        p_hi = [sb(f"p_hi{h}", [P, QT, GQ], f16) for h in range(2)]
        p_lo = [sb(f"p_lo{h}", [P, QT, GQ], f16) for h in range(2)]
        runmax = [sb(f"runmax{h}", [P, GQ], f32) for h in range(2)]
        maxcol = sb("maxcol", [P, GT], f32)
        maxdiag = sb("maxdiag", [P, GT, P], f32)
        maxrow = sb("maxrow", [P, GQ], f32)
        att = [sb(f"att{i}", [P, C], f32) for i in range(2)]

        wqkv = sb("wqkv", [P, 6, C], f32)
        wtmp = sb("wtmp", [P, 6, C], f32)
        wpt = sb("wpt", [P, CK, C], f32)
        nw = sb("nw", [P, C], f32)
        nb_ = sb("nb_", [P, C], f32)
        qkvb = sb("qkvb", [P, 6], f32)
        pb = sb("pb", [P, CK], f32)
        bfold = sb("bfold", [P, 6], f32)
        bq_wide = sb("bq_wide", [P, CK, P], f32)
        m_hi = sb("m_hi", [P, CK, C], f16)
        m_lo = sb("m_lo", [P, CK, C], f16)
        w2_hi = sb("w2_hi", [P, CK, VW], f16)
        w2_lo = sb("w2_lo", [P, CK, VW], f16)
        vecs = sb("vecs", [P, 8], f32)
        bout = sb("bout", [P, CK], f32)
        amax = sb("amax", [P, 4], f32)
        top = sb("top", [P, 2], f32)
        toprec = sb("toprec", [P, 2], f32)
        factor = sb("factor", [P, 2], f32)
        unscale = sb("unscale", [P, 2], f32)
        ident = sb("ident", [P, P], f32)
        ones = sb("ones", [P, P], f32)
        gmean = sb("gmean", [P, P], f32)
        mhalf = sb("mhalf", [P, CK], f32)

        stats = sb("stats", [P, CK, 2, 6], f32)
        chan = sb("chan", [P, CK, 2], f32)
        grp = sb("grp", [P, CK, 2], f32)
        dev = sb("dev", [P, CK], f32)
        dev2 = sb("dev2", [P, CK], f32)
        var = sb("var", [P, CK], f32)
        rstd = sb("rstd", [P, CK], f32)
        ckey = sb("ckey", [P, QT], f32)
        ln_p = sb("ln_p", [P, 1], f32)
        rinv = sb("rinv", [P, QT], f32)

        ps_s = [ctx.enter_context(nc.psum_tensor(f"ps_s{i}", [P, GQ], f32)) for i in range(BANKS)]
        ps_o = [ctx.enter_context(nc.psum_tensor(f"ps_o{i}", [P, 512], f32)) for i in range(2)]
        ps_m = ctx.enter_context(nc.psum_tensor("ps_m", [P, 512], f32))
        ps_x = ctx.enter_context(nc.psum_tensor("ps_x", [P, 512], f32))

        w_loaded = sem("w_loaded")
        x_loaded = sem("x_loaded")
        stored = sem("stored")
        consts = sem("consts")
        ident_ready = sem("ident_ready")
        folded = sem("folded")
        prod_done = sem("prod_done")
        amax_ready = sem("amax_ready")
        top_ready = sem("top_ready")
        w_ready = sem("w_ready")
        dstep = sem("dstep")
        chan_ready = sem("chan_ready")
        gmean_done = sem("gmean_done")
        dev_ready = sem("dev_ready")
        gvar_done = sem("gvar_done")
        var_ready = sem("var_ready")
        rstd_ready = sem("rstd_ready")
        n32_ready = sem("n32_ready")
        nhi_ready = sem("nhi_ready")
        nlo_ready = sem("nlo_ready")
        grp_ready = sem("grp_ready")
        devstep = sem("devstep")
        ones_ready = sem("ones_ready")
        gmean_ready = sem("gmean_ready")
        piece_done = sem("piece_done")
        piece_hi = sem("piece_hi")
        piece_lo = sem("piece_lo")
        c_ready = sem("c_ready")
        scores_done = sem("scores_done")
        copied = sem("copied")
        maxed = sem("maxed")
        maxt_done = sem("maxt_done")
        maxcol_ready = sem("maxcol_ready")
        diag_ready = sem("diag_ready")
        maxb_done = sem("maxb_done")
        maxrow_ready = sem("maxrow_ready")
        shifted = sem("shifted")
        last_shifted = sem("last_shifted")
        prob_ready = sem("prob_ready")
        phi_ready = sem("phi_ready")
        plo_ready = sem("plo_ready")
        values_done = sem("values_done")
        rinv_ready = sem("rinv_ready")
        att_ready = sem("att_ready")
        ot_done = sem("ot_done")
        res_ready = sem("res_ready")

        block = ctx.enter_context(nc.Block())

        def count(b, j):
            return b * QT + (j + 1)

        def tile_count(b, h, k):
            return b * (2 * QT) + (h * QT + k + 1)

        def pair_count(b, h, p):
            return b * (2 * PAIRS) + (h * PAIRS + p + 1)

        def group_count(b, h):
            return b * 2 + (h + 1)

        def piece_count(b, i):
            return b * PIECES + (i + 1)

        class Place:
            def __init__(self, par, ring):
                self.par, self.ring = par, ring

        def places(b, par, eng=None):
            def ring(d):
                if isinstance(b, int):
                    return (b + d) % XRING
                return eng.snap((b + (XRING + d)) & (XRING - 1)) if eng is not None else None
            return {d: Place((par + d) % 2, ring(d)) for d in (-2, -1, 0, 1)}

        def all_batches(eng, batch):
            batch(0, 0, False)
            batch(1, 1, False)
            with eng.Fori(1, B // 2 - 1) as pair:
                for par in range(2):
                    batch(pair * 2 + par, par, False)
            batch(B - 2, 0, False)
            batch(B - 1, 1, True)

        def pieces_at(b, h, k, last, values_at, keys_at):
            if h == 0 and k in values_at:
                return [(0, b, KPIECES + values_at[k])]
            if h == 1 and k in keys_at and not last:
                return [(1, b + 1, keys_at[k])]
            return []

        def pieces_before(b, h, k, last):
            return pieces_at(b, h, k, last, VALUES_BEFORE, KEYS_BEFORE)

        def pieces_behind(b, h, k, last):
            return pieces_at(b, h, k, last, VALUES_BEHIND, KEYS_BEHIND)

        def is_batch(b, n):
            return isinstance(b, int) and b == n

        @block.sync
        def _(sp):
            def load(b, place):
                sp.dma_start(ximg[:, place, :, :], x_v[b]).then_inc(x_loaded, 16)

            def store(b, place, tiles):
                sp.wait_ge(res_ready, tiles)
                sp.dma_start(out_v[b], ximg[:, place, :, :]).then_inc(stored, 16)

            sp.dma_start(wqkv[:, :, :], qkv_w.rearrange("(t p) c -> p t c", p=P)).then_inc(w_loaded, 16)
            sp.dma_start(nw[:, :], norm_w.rearrange("(a c) -> a c", a=1).broadcast_to([P, C])).then_inc(w_loaded, 16)
            sp.dma_start(nb_[:, :], norm_b.rearrange("(a c) -> a c", a=1).broadcast_to([P, C])).then_inc(w_loaded, 16)
            sp.dma_start(qkvb[:, :], qkv_b_cols).then_inc(w_loaded, 16)
            sp.dma_start(pb[:, :], proj_b_cols).then_inc(w_loaded, 16)
            sp.dma_start(wpt[:, :, :], proj_w_t.rearrange("(t p) c -> p t c", p=P)).then_inc(w_loaded, 16)
            for b in range(XRING):
                load(b, b)
                sp.wait_ge(x_loaded, (b + 1) * 16)
            with sp.Fori(0, B - XRING) as b:
                place = sp.snap(b & (XRING - 1))
                tiles = sp.snap((b + 1) * QT)
                earlier = sp.snap(b * 16 + XRING * 16)
                store_count = sp.snap((b << 4) + 16)
                following = sp.snap(b + XRING)
                store(b, place, tiles)
                sp.wait_ge(stored, store_count)
                sp.wait_ge(x_loaded, earlier)
                load(following, place)
            for b in range(B - XRING, B):
                store(b, b % XRING, (b + 1) * QT)
                sp.wait_ge(stored, (b + 1) * 16)

        @block.gpsimd
        def _(pool):
            nc.gpsimd.memset(mhalf[:, :], -0.5).then_inc(consts, 1)
            nc.gpsimd.memset(ln_p[:, :], LN_P).then_inc(consts, 1)
            pool.wait_ge(consts, 4)
            nc.gpsimd.affine_select(out=ident[:, :], in_=ones[:, :], compare_op=ALU.is_equal, fill=0.0, base=0,
                                    pattern=[[-1, P]], channel_multiplier=1).then_inc(ident_ready, 1)
            pool.wait_ge(amax_ready, 1)
            nc.gpsimd.partition_all_reduce(top[:, :], amax[:, 0:2], P, bass.bass_isa.ReduceOp.max).then_inc(top_ready, 1)

            def inverse_deviation(b):
                pool.wait_ge(var_ready, b + 1)
                nc.gpsimd.tensor_tensor(rstd[:, :], var[:, :], mhalf[:, :], ALU.pow).then_inc(rstd_ready, 1)

            def split_low(w, b, h):
                pool.wait_ge(nhi_ready, b * 2 + (h + 1))
                at = slice(h * HALF, (h + 1) * HALF)
                nc.gpsimd.tensor_tensor(n_lo[:, w.par, :, at], norm32[:, :, at], n_hi[:, w.par, :, at],
                                        ALU.subtract).then_inc(nlo_ready, 1)

            def take_maximum(b, h, p):
                if p == 0:
                    pool.wait_ge(maxrow_ready, group_count(b, h))
                two = score[h][:, 2 * p:2 * p + 2, :]
                nc.gpsimd.tensor_tensor(two, two, maxrow[:, :].unsqueeze(1).broadcast_to([P, 2, GQ]),
                                        ALU.subtract).then_inc(shifted, 1)

            def batch(b, par, last):
                w = places(b, par)
                if not is_batch(b, 0):
                    for p in range(PAIRS):
                        take_maximum(b - 1, 1, p)
                if not last:
                    inverse_deviation(b + 1)
                    split_low(w[1], b + 1, 0)
                take_maximum(b, 0, 0)
                take_maximum(b, 0, 1)
                if not last:
                    split_low(w[1], b + 1, 1)
                take_maximum(b, 0, 2)
                take_maximum(b, 0, 3)

            w0 = places(0, 0)
            inverse_deviation(0)
            for h in range(2):
                split_low(w0[0], 0, h)
            all_batches(pool, batch)
            for p in range(0, PAIRS, 2):
                take_maximum(B - 1, 1, p)

        @block.scalar
        def _(act):
            def split_high(w, b, h):
                act.wait_ge(n32_ready, (b + 1) * CK)
                at = slice(h * HALF, (h + 1) * HALF)
                nc.scalar.activation(n_hi[:, w.par, :, at], norm32[:, :, at], ACT.Copy).then_inc(nhi_ready, 1)

            def piece(w, b, i):
                act.wait_ge(piece_done, piece_count(b, i))
                if i < KPIECES:
                    m, h = i % CK, i // CK
                    nc.scalar.activation(t_hi[:, w.par, m, h * HALF:(h + 1) * HALF], ps_x[:, :],
                                         ACT.Identity, bias=vecs[:, m:m + 1]).then_inc(piece_hi, 1)
                else:
                    nc.scalar.activation(v_hi[:, w.par, i - KPIECES, 0:C], ps_x[:, 0:C],
                                         ACT.Copy).then_inc(piece_hi, 1)

            def copy_scores(b, h, k):
                act.wait_ge(scores_done, tile_count(b, h, k))
                if h == 0:
                    act.wait_ge(c_ready, count(b, k))
                nc.scalar.activation(score[h][:, k, :], ps_s[k % BANKS][:, :], ACT.Identity,
                                     bias=ckey[:, k:k + 1]).then_inc(copied, 1)

            def copy_maximum(b, h):
                act.wait_ge(maxb_done, group_count(b, h))
                nc.scalar.activation(maxrow[:, :], ps_m[:, :], ACT.Copy).then_inc(maxrow_ready, 1)

            def exponent(b, h, p):
                two = slice(2 * p, 2 * p + 2)
                if is_batch(b, B - 1) and h == 1 and p % 2:
                    act.wait_ge(last_shifted, p // 2 + 1)
                elif is_batch(b, B - 1) and h == 1:
                    act.wait_ge(shifted, pair_count(b, h, p // 2))
                else:
                    act.wait_ge(shifted, pair_count(b, h, p))
                nc.scalar.activation(score[h][:, two, :], score[h][:, two, :], ACT.Exp, bias=ln_p[:, :],
                                     scale=unscale[:, 0:1]).then_inc(prob_ready, 1)
                act.wait_ge(prob_ready, pair_count(b, h, p))
                nc.scalar.activation(p_hi[h][:, two, :], score[h][:, two, :], ACT.Copy).then_inc(phi_ready, 1)

            def batch(b, par, last):
                first = is_batch(b, 0)
                w = places(b, par)
                for h in range(2):
                    before = (b, 0) if h else (b - 1, 1)
                    softmax = not (first and h == 0)
                    for k in range(QT):
                        if k == 0 and not first:
                            act.wait_ge(plo_ready, pair_count(b - 1, h, PAIRS - 1))
                        for d, of, i in pieces_before(b, h, k, last):
                            piece(w[d], of, i)
                        copy_scores(b, h, k)
                        for d, of, i in pieces_behind(b, h, k, last):
                            piece(w[d], of, i)
                        if h == 1 and k < 2 and not last:
                            split_high(w[1], b + 1, k)
                        if k == 1 and softmax:
                            copy_maximum(*before)
                        if k in EXP_AT and softmax:
                            exponent(*before, EXP_AT[k])

            w0 = places(0, 0)
            for h in range(2):
                split_high(w0[0], 0, h)
            act.wait_ge(w_ready, 1)
            for i in range(KPIECES):
                piece(w0[0], 0, i)
            all_batches(act, batch)
            copy_maximum(B - 1, 1)
            for p in range(PAIRS):
                exponent(B - 1, 1, p)

        @block.vector
        def _(dve):
            steps = [0]

            def link(ins):
                steps[0] += 1
                ins.then_inc(dstep, 1)
                dve.wait_ge(dstep, steps[0])

            V = nc.vector

            def channel_stats(w, b, c):
                if c == 0:
                    dve.wait_ge(x_loaded, (b + 1) * 16)
                for h in range(2):
                    V.bn_stats(stats[:, c, h, :], ximg[:, w.ring, c, h * HALF:(h + 1) * HALF])
                V.drain()
                V.bn_aggr(chan[:, c, :], stats[:, c, :, :].rearrange("p h s -> p (h s)")).then_inc(chan_ready, 1)

            def deviations(b):
                dve.wait_ge(gmean_done, b + 1)
                V.tensor_copy(grp[:, :, :].rearrange("p c s -> p (c s)"), ps_m[:, 0:2 * CK]).then_inc(grp_ready, 1)
                dve.wait_ge(grp_ready, b + 1)
                V.tensor_tensor(dev[:, :], chan[:, :, 0], grp[:, :, 0], ALU.subtract).then_inc(devstep, 1)
                dve.wait_ge(devstep, b + 1)
                V.tensor_tensor(dev2[:, :], dev[:, :], dev[:, :], ALU.mult).then_inc(dev_ready, 1)

            def variance(b):
                dve.wait_ge(gvar_done, b + 1)
                V.scalar_tensor_tensor(out=var[:, :], in0=ps_m[:, 0:CK], scalar=EPS, in1=grp[:, :, 1],
                                       op0=ALU.add, op1=ALU.add).then_inc(var_ready, 1)

            def normalise(w, b):
                dve.wait_ge(rstd_ready, b + 1)
                for c in range(CK):
                    V.tensor_scalar(norm32[:, c, :], ximg[:, w.ring, c, :], grp[:, c, 0:1],
                                    rstd[:, c:c + 1], ALU.subtract, ALU.mult).then_inc(n32_ready, 1)

            def piece(w, b, i):
                if i < KPIECES:
                    dve.wait_ge(piece_hi, piece_count(b, i))
                    m, h = i % CK, i // CK
                    at = slice(h * HALF, (h + 1) * HALF)
                    V.scalar_tensor_tensor(out=t_lo[:, w.par, m, at], in0=ps_x[:, :], scalar=vecs[:, m:m + 1],
                                           in1=t_hi[:, w.par, m, at], op0=ALU.add, op1=ALU.subtract).then_inc(piece_lo, 1)
                else:
                    k = i - KPIECES
                    dve.wait_ge(piece_hi, piece_count(b, i))
                    V.tensor_scalar(ckey[:, k:k + 1], ps_x[:, C:VW], vecs[:, 4:5], None, ALU.add).then_inc(c_ready, 1)
                    V.tensor_tensor(v_lo[:, w.par, k, 0:C], ps_x[:, 0:C], v_hi[:, w.par, k, 0:C], ALU.subtract).then_inc(piece_lo, 1)

            def maximum(b, h, k):
                dve.wait_ge(copied, tile_count(b, h, k))
                if k == 0:
                    V.tensor_scalar(runmax[h][:, :], ps_s[0][:, :], ckey[:, 0:1], None, ALU.add).then_inc(maxed, 1)
                else:
                    dve.wait_ge(maxed, tile_count(b, h, k - 1))
                    V.scalar_tensor_tensor(out=runmax[h][:, :], in0=ps_s[k % BANKS][:, :], scalar=ckey[:, k:k + 1],
                                           in1=runmax[h][:, :], op0=ALU.add, op1=ALU.max).then_inc(maxed, 1)

            def diagonal(b, h):
                dve.wait_ge(maxt_done, group_count(b, h))
                V.tensor_reduce(maxcol[:, :], ps_m[:, :].rearrange("p (t k) -> p t k", t=GT), AX.X, ALU.max) \
                    .then_inc(maxcol_ready, 1)
                dve.wait_ge(maxcol_ready, group_count(b, h))
                V.tensor_tensor(maxdiag[:, :, :], ident[:, :].unsqueeze(1).broadcast_to([P, GT, P]),
                                maxcol[:, :].unsqueeze(2).broadcast_to([P, GT, P]), ALU.mult).then_inc(diag_ready, 1)

            def prob_low(b, h, p):
                two = slice(2 * p, 2 * p + 2)
                dve.wait_ge(phi_ready, pair_count(b, h, p))
                V.tensor_tensor(p_lo[h][:, two, :], score[h][:, two, :], p_hi[h][:, two, :],
                                ALU.subtract).then_inc(plo_ready, 1)

            def take_values(b, j):
                n = count(b, j)
                j = j % QT
                dve.wait_ge(values_done, n)
                V.reciprocal(rinv[:, j:j + 1], ps_o[j % 2][:, C:VW]).then_inc(rinv_ready, 1)
                dve.wait_ge(rinv_ready, n)
                V.tensor_scalar(att[j % 2][:, :], ps_o[j % 2][:, 0:C], rinv[:, j:j + 1], unscale[:, 1:2],
                                ALU.mult, ALU.mult).then_inc(att_ready, 1)

            def residual(w, b, j):
                dve.wait_ge(ot_done, count(b, j))
                j = j % QT
                for c in range(CK):
                    at = slice(j * P, (j + 1) * P)
                    ins = V.scalar_tensor_tensor(out=ximg[:, w.ring, c, at], in0=ps_o[j % 2][:, c * P:(c + 1) * P],
                                                 scalar=bout[:, c:c + 1], in1=ximg[:, w.ring, c, at],
                                                 op0=ALU.add, op1=ALU.add)
                ins.then_inc(res_ready, 1)

            def batch(b, par, last):
                first, second = is_batch(b, 0), is_batch(b, 1)
                w = places(b, par, dve)
                for h in range(2):
                    before = (b, 0) if h else (b - 1, 1)
                    softmax = not (first and h == 0)
                    for k in range(QT):
                        j = h * GT + k // 2 - 1
                        has_values = not first and not (second and j < 0)
                        if k in LOW_AT and softmax:
                            prob_low(*before, LOW_AT[k])
                        if k % 2 == 0 and has_values:
                            take_values(b - 1, j)
                        for d, of, i in pieces_before(b, h, k, last):
                            piece(w[d], of, i)
                        if k == 0 and softmax:
                            diagonal(*before)
                        maximum(b, h, k)
                        for d, of, i in pieces_behind(b, h, k, last):
                            piece(w[d], of, i)
                        if k % 2 == 1 and has_values:
                            residual(w[-1] if j >= 0 else w[-2], b - 1, j)
                        if not last:
                            if h == 0 and k in (0, 1):
                                channel_stats(w[1], b + 1, k)
                            if h == 0 and k == 4:
                                deviations(b + 1)
                            if h == 0 and k == 6:
                                variance(b + 1)
                            if h == 1 and k == 0:
                                normalise(w[1], b + 1)

            V.memset(gmean[:, :], 0.0).then_inc(consts, 1)
            V.memset(ones[:, :], 1.0).then_inc(consts, 1)
            dve.wait_ge(consts, 4)
            for g in range(P // GROUP):
                at = slice(g * GROUP, (g + 1) * GROUP)
                V.memset(gmean[at, at], 1.0 / GROUP).then_inc(gmean_ready, 1)

            dve.wait_ge(w_loaded, 6 * 16)
            for t in range(6):
                V.tensor_tensor(wtmp[:, t, :], wqkv[:, t, :], nb_[:, :], ALU.mult).then_inc(folded, 1)
            dve.wait_ge(folded, 6)
            link(V.tensor_reduce(bfold[:, :], wtmp[:, :, :], AX.X, ALU.add))
            link(V.tensor_tensor(bfold[:, :], bfold[:, :], qkvb[:, :], ALU.add))
            for t in range(6):
                V.tensor_tensor(wqkv[:, t, :], wqkv[:, t, :], nw[:, :], ALU.mult).then_inc(folded, 1)
            for k in range(CK):
                V.tensor_scalar(bq_wide[:, k, :], ones[:, :], bfold[:, k:k + 1], None, ALU.mult).then_inc(folded, 1)

            w0 = places(0, 0)
            for c in range(CK):
                channel_stats(w0[0], 0, c)

            dve.wait_ge(prod_done, 1)
            V.tensor_reduce(amax[:, 0:1], ps_s[0][:, 0:CK * C], AX.X, ALU.max, apply_absolute_value=True) \
                .then_inc(dstep, 1)
            V.tensor_reduce(amax[:, 1:2], ps_s[1][:, 0:CK * C], AX.X, ALU.max, apply_absolute_value=True) \
                .then_inc(dstep, 1)
            V.tensor_reduce(amax[:, 2:3], ps_x[:, 0:2 * CK], AX.X, ALU.max, apply_absolute_value=True) \
                .then_inc(dstep, 1)
            steps[0] += 3
            dve.wait_ge(dstep, steps[0])
            V.scalar_tensor_tensor(out=amax[:, 0:1], in0=amax[:, 2:3], scalar=1.0 / VEC, in1=amax[:, 0:1],
                                   op0=ALU.mult, op1=ALU.max).then_inc(amax_ready, 1)
            dve.wait_ge(top_ready, 1)
            link(V.tensor_scalar(top[:, :], top[:, :], 1e-30, None, ALU.max))
            link(V.reciprocal(toprec[:, :], top[:, :]))
            link(V.tensor_scalar(factor[:, :], toprec[:, :], TOP, None, ALU.mult))
            link(V.tensor_scalar(unscale[:, 0:1], top[:, 0:1], SCALE / TOP, None, ALU.mult))
            link(V.tensor_scalar(unscale[:, 1:2], top[:, 1:2], 1.0 / TOP, None, ALU.mult))
            link(V.tensor_scalar(vecs[:, 0:5], ps_x[:, 0:5], factor[:, 0:1], None, ALU.mult))
            link(V.tensor_tensor(bout[:, :], ps_x[:, 5:5 + CK], pb[:, :], ALU.add))
            m_flat = [m[:, :, :].rearrange("p k c -> p (k c)") for m in (m_hi, m_lo)]
            link(V.tensor_scalar(m_flat[0], ps_s[0][:, 0:CK * C], factor[:, 0:1], None, ALU.mult))
            link(V.scalar_tensor_tensor(out=m_flat[1], in0=ps_s[0][:, 0:CK * C], scalar=factor[:, 0:1],
                                        in1=m_flat[0], op0=ALU.mult, op1=ALU.subtract))
            for k in range(CK):
                link(V.tensor_scalar(w2_hi[:, k, 0:C], ps_s[1][:, k * C:(k + 1) * C], factor[:, 1:2], None, ALU.mult))
                link(V.scalar_tensor_tensor(out=w2_lo[:, k, 0:C], in0=ps_s[1][:, k * C:(k + 1) * C],
                                            scalar=factor[:, 1:2], in1=w2_hi[:, k, 0:C],
                                            op0=ALU.mult, op1=ALU.subtract))
                link(V.tensor_copy(w2_hi[:, k, C:VW], vecs[:, CK + k:CK + k + 1]))
                link(V.tensor_tensor(w2_lo[:, k, C:VW], vecs[:, CK + k:CK + k + 1], w2_hi[:, k, C:VW], ALU.subtract))
            V.tensor_copy(amax[:, 3:4], top[:, 0:1]).then_inc(w_ready, 1)

            for buf, value in ((v_hi, 1.0), (v_lo, 0.0)):
                V.memset(buf[:, :, :, C:VP], value).then_inc(ones_ready, 1)

            deviations(0)
            variance(0)
            normalise(w0[0], 0)
            for i in range(KPIECES):
                piece(w0[0], 0, i)

            all_batches(dve, batch)

            wl = places(B, 0)
            take_values(B - 1, -1)
            diagonal(B - 1, 1)
            residual(wl[-2], B - 1, -1)
            dve.wait_ge(maxrow_ready, group_count(B - 1, 1))
            for p in range(1, PAIRS, 2):
                two = score[1][:, 2 * p:2 * p + 2, :]
                V.tensor_tensor(two, two, maxrow[:, :].unsqueeze(1).broadcast_to([P, 2, GQ]),
                                ALU.subtract).then_inc(last_shifted, 1)
            for p in range(PAIRS):
                prob_low(B - 1, 1, p)
            for j in range(QT):
                take_values(B - 1, j)
                residual(wl[-1], B - 1, j)

        @block.tensor
        def _(pe):
            T = nc.tensor

            def split_product(dst, ah, al, bh, bl, chunks):
                n = 0
                for k in range(chunks):
                    for lhs, rhs in ((ah, bh), (ah, bl), (al, bh)):
                        n += 1
                        last = T.matmul(dst, lhs(k), rhs(k), start=(n == 1), stop=(n == 3 * chunks))
                return last

            def group_means(b):
                pe.wait_ge(chan_ready, (b + 1) * CK)
                T.matmul(ps_m[:, 0:2 * CK], gmean[:, :], chan[:, :, :].rearrange("p c s -> p (c s)"),
                         start=True, stop=True).then_inc(gmean_done, 1)

            def group_deviation(b):
                pe.wait_ge(dev_ready, b + 1)
                T.matmul(ps_m[:, 0:CK], gmean[:, :], dev2[:, :], start=True, stop=True).then_inc(gvar_done, 1)

            def piece(w, b, i):
                if i > 0:
                    pe.wait_ge(piece_lo, piece_count(b, i - 1))
                elif not isinstance(b, int) or b > 0:
                    pe.wait_ge(piece_lo, piece_count(b - 1, PIECES - 1))
                if i < KPIECES:
                    m, h = i % CK, i // CK
                    pe.wait_ge(nlo_ready, b * 2 + (h + 1))
                    at = slice(h * HALF, (h + 1) * HALF)
                    split_product(ps_x[:, :],
                                  lambda k: m_hi[:, k, m * P:(m + 1) * P], lambda k: m_lo[:, k, m * P:(m + 1) * P],
                                  lambda k: n_hi[:, w.par, k, at], lambda k: n_lo[:, w.par, k, at], CK).then_inc(piece_done, 1)
                else:
                    at = slice((i - KPIECES) * P, (i - KPIECES + 1) * P)
                    split_product(ps_x[:, 0:VW],
                                  lambda k: n_hi[:, w.par, k, at], lambda k: n_lo[:, w.par, k, at],
                                  lambda k: w2_hi[:, k, :], lambda k: w2_lo[:, k, :], CK).then_inc(piece_done, 1)

            def scores(w, b, h, k, fresh):
                if not (fresh and k < BANKS):
                    pe.wait_ge(maxed, tile_count(b, h, k - BANKS))
                at = slice(k * P, (k + 1) * P)
                queries = slice(h * GQ, (h + 1) * GQ)
                split_product(ps_s[k % BANKS][:, :],
                              lambda c: t_hi[:, w.par, c, at], lambda c: t_lo[:, w.par, c, at],
                              lambda c: n_hi[:, w.par, c, queries], lambda c: n_lo[:, w.par, c, queries],
                              CK).then_inc(scores_done, 1)

            def transpose_maxima(b, h):
                pe.wait_ge(maxed, tile_count(b, h, QT - 1))
                for t in range(GT):
                    last = T.transpose(ps_m[:, t * P:(t + 1) * P], runmax[h][:, t * P:(t + 1) * P], ident[:, :])
                last.then_inc(maxt_done, 1)

            def spread_maxima(b, h):
                pe.wait_ge(diag_ready, group_count(b, h))
                T.matmul(ps_m[:, :], ones[:, :], maxdiag[:, :, :].rearrange("p t k -> p (t k)"),
                         start=True, stop=True).then_inc(maxb_done, 1)

            def values(w, b, h, i, fresh):
                if i == 0:
                    pe.wait_ge(plo_ready, pair_count(b, h, PAIRS - 1))
                j = h * GT + i
                if not (fresh and j < 2):
                    pe.wait_ge(res_ready, count(b, j - 2))
                n = 0
                for k in range(QT):
                    ph, pl = (buf[h][:, k, i * P:(i + 1) * P] for buf in (p_hi, p_lo))
                    T.matmul(ps_o[j % 2][:, 0:VW], ph, v_hi[:, w.par, k, 0:VW], start=(k == 0), stop=False)
                    T.matmul(ps_o[j % 2][:, 0:C], ph, v_lo[:, w.par, k, 0:C], start=False, stop=False)
                    last = T.matmul(ps_o[j % 2][:, 0:VW], pl, v_hi[:, w.par, k, 0:VW], start=False, stop=(k == QT - 1))
                last.then_inc(values_done, 1)

            def transpose_output(b, j):
                pe.wait_ge(att_ready, count(b, j))
                j = j % QT
                for c in range(CK):
                    last = T.transpose(ps_o[j % 2][:, c * P:(c + 1) * P], att[j % 2][:, c * P:(c + 1) * P], ident[:, :])
                last.then_inc(ot_done, 1)

            def batch(b, par, last):
                first, second = is_batch(b, 0), is_batch(b, 1)
                w = places(b, par)
                for h in range(2):
                    before = (b, 0) if h else (b - 1, 1)
                    softmax = not (first and h == 0)
                    for k in range(QT):
                        for d, of, i in pieces_before(b, h, k, last):
                            piece(w[d], of, i)
                        scores(w[0], b, h, k, first and h == 0)
                        if k == 0 and softmax:
                            if h == 1 and not last:
                                pe.wait_ge(var_ready, b + 2)
                            transpose_maxima(*before)
                        for d, of, i in pieces_behind(b, h, k, last):
                            piece(w[d], of, i)
                        if h == 0 and k == 3 and not last:
                            if not first:
                                pe.wait_ge(maxrow_ready, group_count(b - 1, 1))
                            group_means(b + 1)
                        if h == 0 and k == 5 and not last:
                            group_deviation(b + 1)
                        if k % 2 == 1 and not first:
                            j = h * GT + k // 2 - 1
                            if not (second and j < 0):
                                transpose_output(b - 1, j)
                        if k == 1 and softmax:
                            spread_maxima(*before)
                        if k % 2 == 1 and not first:
                            values(w[-1], b - 1, h, k // 2, second)

            pe.wait_ge(folded, 12 + CK)
            for m in range(CK):
                at = slice(m * P, (m + 1) * P)
                for k in range(CK):
                    T.matmul(ps_s[0][:, m * C:(m + 1) * C], wqkv[:, CK + k, at], wqkv[:, k, :],
                             start=(k == 0), stop=(k == CK - 1))
                for k in range(CK):
                    T.matmul(ps_s[1][:, m * C:(m + 1) * C], wqkv[:, 2 * CK + k, at], wpt[:, k, :],
                             start=(k == 0), stop=(k == CK - 1))
                for col, lhs, bias in ((m, lambda k: wqkv[:, k, at], CK),
                                       (CK + m, lambda k: wqkv[:, CK + k, at], 0),
                                       (5 + m, lambda k: wpt[:, k, at], 2 * CK)):
                    for k in range(CK):
                        T.matmul(ps_x[:, col:col + 1], lhs(k), bfold[:, bias + k:bias + k + 1],
                                 start=(k == 0), stop=(k == CK - 1))
            for k in range(CK):
                last = T.matmul(ps_x[:, 4:5], bq_wide[:, k, :], bfold[:, CK + k:CK + k + 1],
                                start=(k == 0), stop=(k == CK - 1))
            last.then_inc(prod_done, 1)

            pe.wait_ge(gmean_ready, P // GROUP)
            group_means(0)
            group_deviation(0)
            pe.wait_ge(w_ready, 1)
            w0 = places(0, 0)
            for i in range(KPIECES):
                piece(w0[0], 0, i)
            pe.wait_ge(ident_ready, 1)
            pe.wait_ge(ones_ready, 2)

            all_batches(pe, batch)

            wl = places(B, 0)
            transpose_output(B - 1, -1)
            transpose_maxima(B - 1, 1)
            spread_maxima(B - 1, 1)
            for j in range(QT):
                values(wl[-1], B - 1, j // GT, j % GT, False)
                if j > 0:
                    transpose_output(B - 1, j - 1)
            transpose_output(B - 1, QT - 1)


def kernel(x, L0_conv_norm_w, L0_conv_norm_b, L0_conv_qkv_w, L0_conv_qkv_b, L0_conv_proj_w, L0_conv_proj_b):
    import numpy as np
    import concourse.bacc as bacc
    from concourse import mybir as mb
    from concourse.bass_utils import run_bass_kernel_spmd

    nc = bacc.Bacc("TRN2", target_bir_lowering=False, num_devices=1)
    host = {
        "x": x,
        "norm_w": L0_conv_norm_w,
        "norm_b": L0_conv_norm_b,
        "qkv_w": L0_conv_qkv_w,
        "qkv_b": np.asarray(L0_conv_qkv_b).reshape(6, 128).T,
        "proj_w_t": np.asarray(L0_conv_proj_w).T,
        "proj_b": np.asarray(L0_conv_proj_b).reshape(2, 128).T,
    }
    arrays, args = {}, []
    for name, a in host.items():
        a = np.ascontiguousarray(a)
        arrays[f"in_{name}"] = a
        args.append(nc.dram_tensor(f"in_{name}", a.shape, mb.dt.from_np(a.dtype), kind="ExternalInput").ap())
    args.append(nc.dram_tensor("out_0", x.shape, mb.dt.float32, kind="ExternalOutput").ap())
    attention_program(nc, *args)
    r = run_bass_kernel_spmd(nc, [arrays], core_ids=[0])
    return r.results[0]["out_0"]
```

```python
from contextlib import ExitStack

import concourse.bass as bass
from concourse import mybir


def attention_program(nc, x, norm_w, norm_w_cols, norm_b, qkv_w, qkv_b_cols, proj_w_t, proj_b_cols, out):
    f32, f16 = mybir.dt.float32, mybir.dt.float16
    ALU = mybir.AluOpType
    ACT = mybir.ActivationFunctionType
    AX = mybir.AxisListType

    P = 128
    B, C, HH, WW = x.shape
    N = HH * WW
    CK = C // P
    QT = N // P
    HALF_SLOTS = 2
    HALF = N // 2
    GROUP = C // 8
    EPS = 1e-5
    SCALE = float(C) ** -0.5
    TOP = 4.0
    VEC = 4096.0
    LN_P = 6.931471805599453
    VW = C + 1
    VP = VW + 1
    KPIECES = 2 * CK
    PIECES = KPIECES + QT
    GQ = N // HALF_SLOTS
    GT = GQ // P
    PAIRS = QT // 2
    BANKS = 4
    XRING = 4

    VALUES_BEFORE = {0: 0, 2: 3, 4: 5, 6: 7}
    VALUES_BEHIND = {0: 1, 1: 2, 3: 4, 5: 6}
    KEYS_BEFORE = {4: 1, 6: 3}
    KEYS_BEHIND = {3: 0, 5: 2}
    EXP, HIGH = 0, 1
    ACT_AT = {3: ((EXP, 0), (HIGH, 0), (EXP, 1)), 4: ((HIGH, 1),), 5: ((EXP, 2), (HIGH, 2)),
              6: ((EXP, 3),), 7: ((HIGH, 3),)}
    LOW_AT = {4: 0, 5: 1, 6: 2, 7: 3}

    x_v = x.rearrange("b (c p) h w -> b p c (h w)", p=P)
    out_v = out.rearrange("b (c p) h w -> b p c (h w)", p=P)

    ctx = ExitStack()
    with ctx:
        def sb(name, shape, dt):
            return ctx.enter_context(nc.sbuf_tensor(name, shape, dt))

        def sem(name):
            return ctx.enter_context(nc.semaphore(name))

        ximg = sb("ximg", [P, XRING, CK, N], f32)
        norm32 = sb("norm32", [P, CK, N], f32)
        n_hi = sb("n_hi", [P, 2, CK, N], f16)
        n_lo = sb("n_lo", [P, 2, CK, N], f16)
        t_hi = sb("t_hi", [P, 2, CK, N], f16)
        t_lo = sb("t_lo", [P, 2, CK, N], f16)
        v_hi = sb("v_hi", [P, 2, QT, VP], f16)
        v_lo = sb("v_lo", [P, 2, QT, VP], f16)
        score = [sb(f"score{h}", [P, QT, GQ], f32) for h in range(2)]
        p_hi = [sb(f"p_hi{h}", [P, QT, GQ], f16) for h in range(2)]
        p_lo = [sb(f"p_lo{h}", [P, QT, GQ], f16) for h in range(2)]
        runmax = [sb(f"runmax{h}", [P, GQ], f32) for h in range(2)]
        maxcol = sb("maxcol", [P, GT], f32)
        maxrow = sb("maxrow", [P, GQ], f32)
        att = [sb(f"att{i}", [P, C], f32) for i in range(2)]

        wqkv = sb("wqkv", [P, 6, C], f32)
        wnb = sb("wnb", [P, 6, C], f32)
        wpt = sb("wpt", [P, CK, C], f32)
        nw = sb("nw", [P, C], f32)
        nw_cols = sb("nw_cols", [P, 2 * CK + 1], f32)
        m32 = sb("m32", [P, CK, C], f32)
        w32 = sb("w32", [P, CK, C], f32)
        vec32 = sb("vec32", [P, 2 * CK + 1], f32)
        nb_ = sb("nb_", [P, C], f32)
        qkvb = sb("qkvb", [P, 6], f32)
        pb = sb("pb", [P, CK], f32)
        bfold = sb("bfold", [P, 6], f32)
        bq_wide = sb("bq_wide", [P, CK, P], f32)
        m_hi = sb("m_hi", [P, CK, C], f16)
        m_lo = sb("m_lo", [P, CK, C], f16)
        w2_hi = sb("w2_hi", [P, CK, VW], f16)
        w2_lo = sb("w2_lo", [P, CK, VW], f16)
        vecs = sb("vecs", [P, 8], f32)
        bout = sb("bout", [P, CK], f32)
        amax = sb("amax", [P, 3], f32)
        top = sb("top", [P, 2], f32)
        toprec = sb("toprec", [P, 2], f32)
        factor = sb("factor", [P, 2], f32)
        unscale = sb("unscale", [P, 2], f32)
        ident = sb("ident", [P, P], f32)
        ones = sb("ones", [P, P], f32)
        gmean = sb("gmean", [P, P], f32)
        mhalf = sb("mhalf", [P, CK], f32)

        stats = sb("stats", [P, CK, 2, 6], f32)
        chan = sb("chan", [P, CK, 2], f32)
        grp = sb("grp", [P, CK, 2], f32)
        dev = sb("dev", [P, CK], f32)
        dev2 = sb("dev2", [P, CK], f32)
        var = sb("var", [P, CK], f32)
        rstd = sb("rstd", [P, CK], f32)
        ckey = sb("ckey", [P, QT], f32)
        ln_p = sb("ln_p", [P, 1], f32)
        rinv = sb("rinv", [P, QT], f32)

        ps_s = [ctx.enter_context(nc.psum_tensor(f"ps_s{i}", [P, GQ], f32)) for i in range(BANKS)]
        ps_o = [ctx.enter_context(nc.psum_tensor(f"ps_o{i}", [P, 512], f32)) for i in range(2)]
        ps_m = ctx.enter_context(nc.psum_tensor("ps_m", [P, 512], f32))
        ps_x = ctx.enter_context(nc.psum_tensor("ps_x", [P, 512], f32))

        qkv_loaded = sem("qkv_loaded")
        projw_loaded = sem("projw_loaded")
        nb_loaded = sem("nb_loaded")
        small_loaded = sem("small_loaded")
        x_loaded = sem("x_loaded")
        stored = sem("stored")
        consts = sem("consts")
        ident_ready = sem("ident_ready")
        biases_ready = sem("biases_ready")
        m_done = sem("m_done")
        w2_done = sem("w2_done")
        vec_done = sem("vec_done")
        w32_ready = sem("w32_ready")
        scale_ready = sem("scale_ready")
        whi_ready = sem("whi_ready")
        amax_ready = sem("amax_ready")
        top_ready = sem("top_ready")
        w_ready = sem("w_ready")
        dstep = sem("dstep")
        chan_ready = sem("chan_ready")
        gmean_done = sem("gmean_done")
        dev_ready = sem("dev_ready")
        gvar_done = sem("gvar_done")
        var_ready = sem("var_ready")
        rstd_ready = sem("rstd_ready")
        n32_ready = sem("n32_ready")
        nhi_ready = sem("nhi_ready")
        nlo_ready = sem("nlo_ready")
        grp_ready = sem("grp_ready")
        devstep = sem("devstep")
        ones_ready = sem("ones_ready")
        gmean_ready = sem("gmean_ready")
        piece_done = sem("piece_done")
        piece_hi = sem("piece_hi")
        piece_lo = sem("piece_lo")
        c_ready = sem("c_ready")
        scores_done = sem("scores_done")
        copied = sem("copied")
        maxed = sem("maxed")
        maxt_done = sem("maxt_done")
        maxcol_ready = sem("maxcol_ready")
        maxb_done = sem("maxb_done")
        maxrow_ready = sem("maxrow_ready")
        shifted = sem("shifted")
        last_shifted = sem("last_shifted")
        prob_ready = sem("prob_ready")
        phi_ready = sem("phi_ready")
        plo_ready = sem("plo_ready")
        values_done = sem("values_done")
        rinv_ready = sem("rinv_ready")
        att_ready = sem("att_ready")
        ot_done = sem("ot_done")
        res_ready = sem("res_ready")

        block = ctx.enter_context(nc.Block())

        def count(b, j):
            return b * QT + (j + 1)

        def tile_count(b, h, k):
            return b * (2 * QT) + (h * QT + k + 1)

        def pair_count(b, h, p):
            return b * (2 * PAIRS) + (h * PAIRS + p + 1)

        def group_count(b, h):
            return b * 2 + (h + 1)

        def piece_count(b, i):
            return b * PIECES + (i + 1)

        class Place:
            def __init__(self, par, ring):
                self.par, self.ring = par, ring

        def places(b, par, eng=None):
            def ring(d):
                if isinstance(b, int):
                    return (b + d) % XRING
                return eng.snap((b + (XRING + d)) & (XRING - 1)) if eng is not None else None
            return {d: Place((par + d) % 2, ring(d)) for d in (-2, -1, 0, 1)}

        def all_batches(eng, batch):
            batch(0, 0, False)
            batch(1, 1, False)
            with eng.Fori(1, B // 2 - 1) as pair:
                for par in range(2):
                    batch(pair * 2 + par, par, False)
            batch(B - 2, 0, False)
            batch(B - 1, 1, True)

        def pieces_at(b, h, k, last, values_at, keys_at):
            if h == 0 and k in values_at:
                return [(0, b, KPIECES + values_at[k])]
            if h == 1 and k in keys_at and not last:
                return [(1, b + 1, keys_at[k])]
            return []

        def pieces_before(b, h, k, last):
            return pieces_at(b, h, k, last, VALUES_BEFORE, KEYS_BEFORE)

        def pieces_behind(b, h, k, last):
            return pieces_at(b, h, k, last, VALUES_BEHIND, KEYS_BEHIND)

        def piece_bank(b, i):
            if not is_batch(b, 0):
                return ps_x
            return (ps_o[0], ps_o[1], ps_m, ps_x)[i] if i < KPIECES else (ps_o[0], ps_o[1], ps_x)[(i - KPIECES) % 3]

        def is_batch(b, n):
            return isinstance(b, int) and b == n

        @block.sync
        def _(sp):
            def load(b, place):
                sp.dma_start(ximg[:, place, :, :], x_v[b]).then_inc(x_loaded, 16)

            def store(b, place, tiles):
                sp.wait_ge(res_ready, tiles)
                sp.dma_start(out_v[b], ximg[:, place, :, :]).then_inc(stored, 16)

            sp.dma_start(wqkv[:, :, :], qkv_w.rearrange("(t p) c -> p t c", p=P)).then_inc(qkv_loaded, 16)
            sp.dma_start(nb_[:, :], norm_b.rearrange("(a c) -> a c", a=1).broadcast_to([P, C])).then_inc(nb_loaded, 16)
            sp.dma_start(wpt[:, :, :], proj_w_t.rearrange("(t p) c -> p t c", p=P)).then_inc(projw_loaded, 16)
            sp.dma_start(qkvb[:, :], qkv_b_cols).then_inc(small_loaded, 16)
            load(0, 0)
            sp.dma_start(nw[:, :], norm_w.rearrange("(a c) -> a c", a=1).broadcast_to([P, C])).then_inc(small_loaded, 16)
            for i in range(2):
                sp.dma_start(nw_cols[:, i * CK:(i + 1) * CK], norm_w_cols).then_inc(small_loaded, 16)
            sp.dma_start(pb[:, :], proj_b_cols).then_inc(small_loaded, 16)
            sp.wait_ge(x_loaded, 16)
            for b in range(1, XRING):
                load(b, b)
                sp.wait_ge(x_loaded, (b + 1) * 16)
            with sp.Fori(0, B - XRING) as b:
                place = sp.snap(b & (XRING - 1))
                tiles = sp.snap((b + 1) * QT)
                earlier = sp.snap(b * 16 + XRING * 16)
                store_count = sp.snap((b << 4) + 16)
                following = sp.snap(b + XRING)
                store(b, place, tiles)
                sp.wait_ge(stored, store_count)
                sp.wait_ge(x_loaded, earlier)
                load(following, place)
            for b in range(B - XRING, B):
                store(b, b % XRING, (b + 1) * QT)
                sp.wait_ge(stored, (b + 1) * 16)

        @block.gpsimd
        def _(pool):
            nc.gpsimd.memset(mhalf[:, :], -0.5).then_inc(consts, 1)
            nc.gpsimd.memset(ln_p[:, :], LN_P).then_inc(consts, 1)
            pool.wait_ge(consts, 4)
            nc.gpsimd.affine_select(out=ident[:, :], in_=ones[:, :], compare_op=ALU.is_equal, fill=0.0, base=0,
                                    pattern=[[-1, P]], channel_multiplier=1).then_inc(ident_ready, 1)
            pool.wait_ge(amax_ready, 1)
            nc.gpsimd.partition_all_reduce(top[:, :], amax[:, 0:2], P, bass.bass_isa.ReduceOp.max).then_inc(top_ready, 1)

            def inverse_deviation(b):
                pool.wait_ge(var_ready, b + 1)
                nc.gpsimd.tensor_tensor(rstd[:, :], var[:, :], mhalf[:, :], ALU.pow).then_inc(rstd_ready, 1)

            def split_low(w, b, h):
                pool.wait_ge(nhi_ready, b * 2 + (h + 1))
                at = slice(h * HALF, (h + 1) * HALF)
                nc.gpsimd.tensor_tensor(n_lo[:, w.par, :, at], norm32[:, :, at], n_hi[:, w.par, :, at],
                                        ALU.subtract).then_inc(nlo_ready, 1)

            def take_maximum(b, h, p):
                if p == 0:
                    pool.wait_ge(maxrow_ready, group_count(b, h))
                two = score[h][:, 2 * p:2 * p + 2, :]
                nc.gpsimd.tensor_tensor(two, two, maxrow[:, :].unsqueeze(1).broadcast_to([P, 2, GQ]),
                                        ALU.subtract).then_inc(shifted, 1)

            def batch(b, par, last):
                w = places(b, par)
                if not is_batch(b, 0):
                    for p in range(PAIRS):
                        take_maximum(b - 1, 1, p)
                if not last:
                    inverse_deviation(b + 1)
                    split_low(w[1], b + 1, 0)
                take_maximum(b, 0, 0)
                take_maximum(b, 0, 1)
                if not last:
                    split_low(w[1], b + 1, 1)
                take_maximum(b, 0, 2)
                take_maximum(b, 0, 3)

            inverse_deviation(0)
            all_batches(pool, batch)
            for p in range(0, PAIRS, 2):
                take_maximum(B - 1, 1, p)

        @block.scalar
        def _(act):
            def split_high(w, b, h):
                act.wait_ge(n32_ready, h + 1 if is_batch(b, 0) else (b + 1) * CK)
                at = slice(h * HALF, (h + 1) * HALF)
                nc.scalar.activation(n_hi[:, w.par, :, at], norm32[:, :, at], ACT.Copy).then_inc(nhi_ready, 1)

            def piece(w, b, i):
                act.wait_ge(piece_done, piece_count(b, i))
                bank = piece_bank(b, i)
                if i < KPIECES:
                    m, h = i % CK, i // CK
                    nc.scalar.activation(t_hi[:, w.par, m, h * HALF:(h + 1) * HALF], bank[:, :],
                                         ACT.Identity, bias=vecs[:, m:m + 1]).then_inc(piece_hi, 1)
                else:
                    nc.scalar.activation(v_hi[:, w.par, i - KPIECES, 0:C], bank[:, 0:C],
                                         ACT.Copy).then_inc(piece_hi, 1)

            def copy_scores(b, h, k):
                act.wait_ge(scores_done, tile_count(b, h, k))
                if h == 0:
                    act.wait_ge(c_ready, count(b, k))
                nc.scalar.activation(score[h][:, k, :], ps_s[k % BANKS][:, :], ACT.Identity,
                                     bias=ckey[:, k:k + 1]).then_inc(copied, 1)

            def copy_maximum(b, h):
                act.wait_ge(maxb_done, group_count(b, h))
                nc.scalar.activation(maxrow[:, :], ps_m[:, :], ACT.Copy).then_inc(maxrow_ready, 1)

            def exponent(b, h, p):
                two = slice(2 * p, 2 * p + 2)
                if is_batch(b, B - 1) and h == 1 and p % 2:
                    act.wait_ge(last_shifted, p // 2 + 1)
                elif is_batch(b, B - 1) and h == 1:
                    act.wait_ge(shifted, pair_count(b, h, p // 2))
                else:
                    act.wait_ge(shifted, pair_count(b, h, p))
                nc.scalar.activation(score[h][:, two, :], score[h][:, two, :], ACT.Exp, bias=ln_p[:, :],
                                     scale=unscale[:, 0:1]).then_inc(prob_ready, 1)

            def probability_high(b, h, p):
                two = slice(2 * p, 2 * p + 2)
                act.wait_ge(prob_ready, pair_count(b, h, p))
                nc.scalar.activation(p_hi[h][:, two, :], score[h][:, two, :], ACT.Copy).then_inc(phi_ready, 1)

            def batch(b, par, last):
                first = is_batch(b, 0)
                w = places(b, par)
                for h in range(2):
                    before = (b, 0) if h else (b - 1, 1)
                    softmax = not (first and h == 0)
                    for k in range(QT):
                        if k == 0 and not first:
                            act.wait_ge(plo_ready, pair_count(b - 1, h, PAIRS - 1))
                        for d, of, i in pieces_before(b, h, k, last):
                            piece(w[d], of, i)
                        copy_scores(b, h, k)
                        for d, of, i in pieces_behind(b, h, k, last):
                            piece(w[d], of, i)
                        if h == 1 and k < 2 and not last:
                            split_high(w[1], b + 1, k)
                        if k == 1 and softmax:
                            copy_maximum(*before)
                        if softmax:
                            for kind, pair in ACT_AT.get(k, ()):
                                (exponent, probability_high)[kind](*before, pair)

            act.wait_ge(w2_done, 1)
            act.wait_ge(small_loaded, 5 * 16)
            for k in range(CK):
                nc.scalar.activation(w32[:, k, :], ps_s[1][:, k * C:(k + 1) * C], ACT.Copy,
                                     scale=nw_cols[:, k:k + 1]).then_inc(w32_ready, 1)
            act.wait_ge(scale_ready, 1)
            nc.scalar.activation(m_hi[:, :, :], m32[:, :, :], ACT.Copy, scale=factor[:, 0:1]).then_inc(whi_ready, 1)
            w0 = places(0, 0)
            for h in range(2):
                split_high(w0[0], 0, h)
            nc.scalar.activation(w2_hi[:, :, 0:C], w32[:, :, :], ACT.Copy, scale=factor[:, 1:2]).then_inc(whi_ready, 1)
            act.wait_ge(w_ready, 1)
            for i in range(KPIECES):
                piece(w0[0], 0, i)
            all_batches(act, batch)
            copy_maximum(B - 1, 1)
            for p in range(PAIRS):
                exponent(B - 1, 1, p)
                probability_high(B - 1, 1, p)

        @block.vector
        def _(dve):
            steps = [0]

            def step(ins):
                steps[0] += 1
                ins.then_inc(dstep, 1)

            def settle():
                dve.wait_ge(dstep, steps[0])

            V = nc.vector

            def channel_stats(w, b, c):
                if c == 0:
                    dve.wait_ge(x_loaded, (b + 1) * 16)
                for h in range(2):
                    V.bn_stats(stats[:, c, h, :], ximg[:, w.ring, c, h * HALF:(h + 1) * HALF])
                V.drain()
                V.bn_aggr(chan[:, c, :], stats[:, c, :, :].rearrange("p h s -> p (h s)")).then_inc(chan_ready, 1)

            def deviations(b):
                dve.wait_ge(gmean_done, b + 1)
                V.tensor_copy(grp[:, :, :].rearrange("p c s -> p (c s)"), ps_m[:, 0:2 * CK]).then_inc(grp_ready, 1)
                dve.wait_ge(grp_ready, b + 1)
                V.tensor_tensor(dev[:, :], chan[:, :, 0], grp[:, :, 0], ALU.subtract).then_inc(devstep, 1)
                dve.wait_ge(devstep, b + 1)
                V.tensor_tensor(dev2[:, :], dev[:, :], dev[:, :], ALU.mult).then_inc(dev_ready, 1)

            def variance(b):
                dve.wait_ge(gvar_done, b + 1)
                V.scalar_tensor_tensor(out=var[:, :], in0=ps_m[:, 0:CK], scalar=EPS, in1=grp[:, :, 1],
                                       op0=ALU.add, op1=ALU.add).then_inc(var_ready, 1)

            def normalise(w, b):
                dve.wait_ge(rstd_ready, b + 1)
                for c in range(CK):
                    V.tensor_scalar(norm32[:, c, :], ximg[:, w.ring, c, :], grp[:, c, 0:1],
                                    rstd[:, c:c + 1], ALU.subtract, ALU.mult).then_inc(n32_ready, 1)

            def piece(w, b, i):
                dve.wait_ge(piece_hi, piece_count(b, i))
                bank = piece_bank(b, i)
                if i < KPIECES:
                    m, h = i % CK, i // CK
                    at = slice(h * HALF, (h + 1) * HALF)
                    V.scalar_tensor_tensor(out=t_lo[:, w.par, m, at], in0=bank[:, :], scalar=vecs[:, m:m + 1],
                                           in1=t_hi[:, w.par, m, at], op0=ALU.add, op1=ALU.subtract).then_inc(piece_lo, 1)
                else:
                    k = i - KPIECES
                    V.tensor_scalar(ckey[:, k:k + 1], bank[:, C:VW], vecs[:, 4:5], None, ALU.add).then_inc(c_ready, 1)
                    V.tensor_tensor(v_lo[:, w.par, k, 0:C], bank[:, 0:C], v_hi[:, w.par, k, 0:C],
                                    ALU.subtract).then_inc(piece_lo, 1)

            def maximum(b, h, k):
                dve.wait_ge(copied, tile_count(b, h, k))
                if k == 0:
                    V.tensor_scalar(runmax[h][:, :], ps_s[0][:, :], ckey[:, 0:1], None, ALU.add).then_inc(maxed, 1)
                else:
                    dve.wait_ge(maxed, tile_count(b, h, k - 1))
                    V.scalar_tensor_tensor(out=runmax[h][:, :], in0=ps_s[k % BANKS][:, :], scalar=ckey[:, k:k + 1],
                                           in1=runmax[h][:, :], op0=ALU.add, op1=ALU.max).then_inc(maxed, 1)

            def reduce_maxima(b, h):
                dve.wait_ge(maxt_done, group_count(b, h))
                V.tensor_reduce(maxcol[:, :], ps_m[:, :].rearrange("p (t k) -> p t k", t=GT), AX.X, ALU.max) \
                    .then_inc(maxcol_ready, 1)

            def prob_low(b, h, p):
                two = slice(2 * p, 2 * p + 2)
                dve.wait_ge(phi_ready, pair_count(b, h, p))
                V.tensor_tensor(p_lo[h][:, two, :], score[h][:, two, :], p_hi[h][:, two, :],
                                ALU.subtract).then_inc(plo_ready, 1)

            def take_values(b, j):
                n = count(b, j)
                j = j % QT
                dve.wait_ge(values_done, n)
                V.reciprocal(rinv[:, j:j + 1], ps_o[j % 2][:, C:VW]).then_inc(rinv_ready, 1)
                dve.wait_ge(rinv_ready, n)
                V.tensor_scalar(att[j % 2][:, :], ps_o[j % 2][:, 0:C], rinv[:, j:j + 1], unscale[:, 1:2],
                                ALU.mult, ALU.mult).then_inc(att_ready, 1)

            def residual(w, b, j):
                dve.wait_ge(ot_done, count(b, j))
                j = j % QT
                for c in range(CK):
                    at = slice(j * P, (j + 1) * P)
                    ins = V.scalar_tensor_tensor(out=ximg[:, w.ring, c, at], in0=ps_o[j % 2][:, c * P:(c + 1) * P],
                                                 scalar=bout[:, c:c + 1], in1=ximg[:, w.ring, c, at],
                                                 op0=ALU.add, op1=ALU.add)
                ins.then_inc(res_ready, 1)

            def batch(b, par, last):
                first, second = is_batch(b, 0), is_batch(b, 1)
                w = places(b, par, dve)
                for h in range(2):
                    before = (b, 0) if h else (b - 1, 1)
                    softmax = not (first and h == 0)
                    for k in range(QT):
                        j = h * GT + k // 2 - 1
                        has_values = not first and not (second and j < 0)
                        if k % 2 == 0 and has_values:
                            take_values(b - 1, j)
                        for d, of, i in pieces_before(b, h, k, last):
                            piece(w[d], of, i)
                        if k == 0 and softmax:
                            reduce_maxima(*before)
                        maximum(b, h, k)
                        for d, of, i in pieces_behind(b, h, k, last):
                            piece(w[d], of, i)
                        if k % 2 == 1 and has_values:
                            residual(w[-1] if j >= 0 else w[-2], b - 1, j)
                        if not last:
                            if h == 0 and k in (0, 1):
                                channel_stats(w[1], b + 1, k)
                            if h == 0 and k == 4:
                                deviations(b + 1)
                            if h == 0 and k == 7:
                                variance(b + 1)
                            if h == 1 and k == 0:
                                normalise(w[1], b + 1)
                        if k in LOW_AT and softmax:
                            prob_low(*before, LOW_AT[k])

            V.memset(gmean[:, :], 0.0).then_inc(consts, 1)
            V.memset(ones[:, :], 1.0).then_inc(consts, 1)
            dve.wait_ge(consts, 4)
            for g in range(P // GROUP):
                at = slice(g * GROUP, (g + 1) * GROUP)
                V.memset(gmean[at, at], 1.0 / GROUP).then_inc(gmean_ready, 1)

            for buf, value in ((v_hi, 1.0), (v_lo, 0.0)):
                V.memset(buf[:, :, :, C:VP], value).then_inc(ones_ready, 1)
            step(V.memset(nw_cols[:, 2 * CK:], 1.0))

            dve.wait_ge(qkv_loaded, 16)
            dve.wait_ge(nb_loaded, 16)
            step(V.tensor_tensor(wnb[:, :, :], wqkv[:, :, :], nb_[:, :].unsqueeze(1).broadcast_to([P, 6, C]), ALU.mult))
            settle()
            step(V.tensor_reduce(bfold[:, :], wnb[:, :, :], AX.X, ALU.add))
            settle()
            dve.wait_ge(small_loaded, 5 * 16)
            step(V.tensor_tensor(bfold[:, :], bfold[:, :], qkvb[:, :], ALU.add))
            settle()
            for k in range(CK):
                V.tensor_scalar(bq_wide[:, k, :], ones[:, :], bfold[:, k:k + 1], None, ALU.mult) \
                    .then_inc(biases_ready, 1)

            w0 = places(0, 0)
            for c in range(CK):
                channel_stats(w0[0], 0, c)

            dve.wait_ge(m_done, 1)
            for k in range(CK):
                step(V.scalar_tensor_tensor(out=m32[:, k, :], in0=ps_s[0][:, k * C:(k + 1) * C],
                                            scalar=nw_cols[:, k:k + 1], in1=nw[:, :], op0=ALU.mult, op1=ALU.mult))
            dve.wait_ge(vec_done, 1)
            step(V.tensor_tensor(vec32[:, :], ps_x[:, 0:2 * CK + 1], nw_cols[:, :], ALU.mult))
            step(V.tensor_tensor(bout[:, :], ps_x[:, 5:5 + CK], pb[:, :], ALU.add))
            deviations(0)
            settle()
            step(V.tensor_reduce(amax[:, 0:1], m32[:, :, :].rearrange("p k c -> p (k c)"), AX.X, ALU.max,
                                 apply_absolute_value=True))
            step(V.tensor_reduce(amax[:, 2:3], vec32[:, 0:2 * CK], AX.X, ALU.max, apply_absolute_value=True))
            variance(0)
            dve.wait_ge(w32_ready, CK)
            step(V.tensor_reduce(amax[:, 1:2], w32[:, :, :].rearrange("p k c -> p (k c)"), AX.X, ALU.max,
                                 apply_absolute_value=True))
            settle()
            V.scalar_tensor_tensor(out=amax[:, 0:1], in0=amax[:, 2:3], scalar=1.0 / VEC, in1=amax[:, 0:1],
                                   op0=ALU.mult, op1=ALU.max).then_inc(amax_ready, 1)

            dve.wait_ge(rstd_ready, 1)
            for h in range(2):
                at = slice(h * HALF, (h + 1) * HALF)
                for c in range(CK):
                    last = V.tensor_scalar(norm32[:, c, at], ximg[:, 0, c, at], grp[:, c, 0:1],
                                           rstd[:, c:c + 1], ALU.subtract, ALU.mult)
                last.then_inc(n32_ready, 1)

            dve.wait_ge(top_ready, 1)
            step(V.tensor_scalar(top[:, :], top[:, :], 1e-30, None, ALU.max))
            settle()
            step(V.reciprocal(toprec[:, :], top[:, :]))
            step(V.tensor_scalar(unscale[:, 0:1], top[:, 0:1], SCALE / TOP, None, ALU.mult))
            step(V.tensor_scalar(unscale[:, 1:2], top[:, 1:2], 1.0 / TOP, None, ALU.mult))
            settle()
            V.tensor_scalar(factor[:, :], toprec[:, :], TOP, None, ALU.mult).then_inc(scale_ready, 1)
            dve.wait_ge(scale_ready, 1)
            step(V.tensor_scalar(vecs[:, 0:5], vec32[:, :], factor[:, 0:1], None, ALU.mult))

            dve.wait_ge(whi_ready, 1)
            V.scalar_tensor_tensor(out=m_lo[:, :, :].rearrange("p k c -> p (k c)"),
                                   in0=m32[:, :, :].rearrange("p k c -> p (k c)"), scalar=factor[:, 0:1],
                                   in1=m_hi[:, :, :].rearrange("p k c -> p (k c)"),
                                   op0=ALU.mult, op1=ALU.subtract).then_inc(w_ready, 1)
            for h in range(2):
                at = slice(h * HALF, (h + 1) * HALF)
                dve.wait_ge(nhi_ready, h + 1)
                V.tensor_tensor(n_lo[:, 0, :, at], norm32[:, :, at], n_hi[:, 0, :, at], ALU.subtract) \
                    .then_inc(nlo_ready, 1)

            settle()
            c_cols = vecs[:, CK:2 * CK].unsqueeze(2)
            step(V.tensor_copy(w2_hi[:, :, C:VW], c_cols))
            dve.wait_ge(whi_ready, 2)
            V.scalar_tensor_tensor(out=w2_lo[:, :, 0:C], in0=w32[:, :, :], scalar=factor[:, 1:2],
                                   in1=w2_hi[:, :, 0:C], op0=ALU.mult, op1=ALU.subtract)
            settle()
            V.tensor_tensor(w2_lo[:, :, C:VW], c_cols, w2_hi[:, :, C:VW], ALU.subtract).then_inc(w_ready, 1)

            for i in range(KPIECES):
                piece(w0[0], 0, i)

            all_batches(dve, batch)

            wl = places(B, 0)
            take_values(B - 1, -1)
            reduce_maxima(B - 1, 1)
            residual(wl[-2], B - 1, -1)
            dve.wait_ge(maxrow_ready, group_count(B - 1, 1))
            for p in range(1, PAIRS, 2):
                two = score[1][:, 2 * p:2 * p + 2, :]
                V.tensor_tensor(two, two, maxrow[:, :].unsqueeze(1).broadcast_to([P, 2, GQ]),
                                ALU.subtract).then_inc(last_shifted, 1)
            for p in range(PAIRS):
                prob_low(B - 1, 1, p)
            for j in range(QT):
                take_values(B - 1, j)
                residual(wl[-1], B - 1, j)

        @block.tensor
        def _(pe):
            T = nc.tensor

            def split_product(dst, ah, al, bh, bl, chunks):
                n = 0
                for k in range(chunks):
                    for lhs, rhs in ((ah, bh), (ah, bl), (al, bh)):
                        n += 1
                        last = T.matmul(dst, lhs(k), rhs(k), start=(n == 1), stop=(n == 3 * chunks))
                return last

            def group_means(b):
                pe.wait_ge(chan_ready, (b + 1) * CK)
                T.matmul(ps_m[:, 0:2 * CK], gmean[:, :], chan[:, :, :].rearrange("p c s -> p (c s)"),
                         start=True, stop=True).then_inc(gmean_done, 1)

            def group_deviation(b):
                pe.wait_ge(dev_ready, b + 1)
                T.matmul(ps_m[:, 0:CK], gmean[:, :], dev2[:, :], start=True, stop=True).then_inc(gvar_done, 1)

            def piece(w, b, i):
                if is_batch(b, 0) and i < KPIECES:
                    pass
                elif is_batch(b, 0):
                    pe.wait_ge(piece_lo, piece_count(b, i - 4 if i < KPIECES + 2 else i - 3))
                elif i > 0:
                    pe.wait_ge(piece_lo, piece_count(b, i - 1))
                else:
                    pe.wait_ge(piece_lo, piece_count(b - 1, PIECES - 1))
                bank = piece_bank(b, i)
                if i < KPIECES:
                    m, h = i % CK, i // CK
                    pe.wait_ge(nlo_ready, b * 2 + (h + 1))
                    at = slice(h * HALF, (h + 1) * HALF)
                    split_product(bank[:, :],
                                  lambda k: m_hi[:, k, m * P:(m + 1) * P], lambda k: m_lo[:, k, m * P:(m + 1) * P],
                                  lambda k: n_hi[:, w.par, k, at], lambda k: n_lo[:, w.par, k, at], CK).then_inc(piece_done, 1)
                else:
                    at = slice((i - KPIECES) * P, (i - KPIECES + 1) * P)
                    split_product(bank[:, 0:VW],
                                  lambda k: n_hi[:, w.par, k, at], lambda k: n_lo[:, w.par, k, at],
                                  lambda k: w2_hi[:, k, :], lambda k: w2_lo[:, k, :], CK).then_inc(piece_done, 1)

            def scores(w, b, h, k, fresh):
                if not (fresh and k < BANKS):
                    pe.wait_ge(maxed, tile_count(b, h, k - BANKS))
                at = slice(k * P, (k + 1) * P)
                queries = slice(h * GQ, (h + 1) * GQ)
                split_product(ps_s[k % BANKS][:, :],
                              lambda c: t_hi[:, w.par, c, at], lambda c: t_lo[:, w.par, c, at],
                              lambda c: n_hi[:, w.par, c, queries], lambda c: n_lo[:, w.par, c, queries],
                              CK).then_inc(scores_done, 1)

            def transpose_maxima(b, h):
                pe.wait_ge(maxed, tile_count(b, h, QT - 1))
                for t in range(GT):
                    last = T.transpose(ps_m[:, t * P:(t + 1) * P], runmax[h][:, t * P:(t + 1) * P], ident[:, :])
                last.then_inc(maxt_done, 1)

            def spread_maxima(b, h):
                pe.wait_ge(maxcol_ready, group_count(b, h))
                for t in range(GT):
                    last = T.transpose(ps_m[:, t * P:(t + 1) * P], maxcol[:, t:t + 1].broadcast_to([P, P]), ident[:, :])
                last.then_inc(maxb_done, 1)

            def values(w, b, h, i, fresh):
                if i == 0:
                    pe.wait_ge(plo_ready, pair_count(b, h, PAIRS - 1))
                j = h * GT + i
                if not (fresh and j < 2):
                    pe.wait_ge(res_ready, count(b, j - 2))
                n = 0
                for k in range(QT):
                    ph, pl = (buf[h][:, k, i * P:(i + 1) * P] for buf in (p_hi, p_lo))
                    T.matmul(ps_o[j % 2][:, 0:VW], ph, v_hi[:, w.par, k, 0:VW], start=(k == 0), stop=False)
                    T.matmul(ps_o[j % 2][:, 0:C], ph, v_lo[:, w.par, k, 0:C], start=False, stop=False)
                    last = T.matmul(ps_o[j % 2][:, 0:VW], pl, v_hi[:, w.par, k, 0:VW], start=False, stop=(k == QT - 1))
                last.then_inc(values_done, 1)

            def transpose_output(b, j):
                pe.wait_ge(att_ready, count(b, j))
                j = j % QT
                for c in range(CK):
                    last = T.transpose(ps_o[j % 2][:, c * P:(c + 1) * P], att[j % 2][:, c * P:(c + 1) * P], ident[:, :])
                last.then_inc(ot_done, 1)

            def batch(b, par, last):
                first, second = is_batch(b, 0), is_batch(b, 1)
                w = places(b, par)
                for h in range(2):
                    before = (b, 0) if h else (b - 1, 1)
                    softmax = not (first and h == 0)
                    for k in range(QT):
                        for d, of, i in pieces_before(b, h, k, last):
                            piece(w[d], of, i)
                        if first and h == 0 and k == 0:
                            pe.wait_ge(piece_lo, KPIECES)
                        scores(w[0], b, h, k, first and h == 0)
                        if k == 0 and softmax:
                            if h == 1 and not last:
                                pe.wait_ge(var_ready, b + 2)
                            transpose_maxima(*before)
                        for d, of, i in pieces_behind(b, h, k, last):
                            piece(w[d], of, i)
                        if h == 0 and k == 3 and not last:
                            if not first:
                                pe.wait_ge(maxrow_ready, group_count(b - 1, 1))
                            group_means(b + 1)
                        if h == 0 and k == 6 and not last:
                            group_deviation(b + 1)
                        if k % 2 == 1 and not first:
                            j = h * GT + k // 2 - 1
                            if not (second and j < 0):
                                transpose_output(b - 1, j)
                        if k == 1 and softmax:
                            spread_maxima(*before)
                        if k % 2 == 1 and not first:
                            values(w[-1], b - 1, h, k // 2, second)

            pe.wait_ge(qkv_loaded, 16)
            for bank, first, rhs, done in ((ps_s[0], CK, wqkv, m_done), (ps_s[1], 2 * CK, wpt, w2_done)):
                if rhs is wpt:
                    pe.wait_ge(projw_loaded, 16)
                for m in range(CK):
                    for k in range(CK):
                        last = T.matmul(bank[:, m * C:(m + 1) * C], wqkv[:, first + k, m * P:(m + 1) * P],
                                        rhs[:, k, :], start=(k == 0), stop=(k == CK - 1))
                last.then_inc(done, 1)
            pe.wait_ge(biases_ready, CK)
            for m in range(CK):
                at = slice(m * P, (m + 1) * P)
                for col, lhs, bias in ((m, lambda k: wqkv[:, k, at], CK),
                                       (CK + m, lambda k: wqkv[:, CK + k, at], 0),
                                       (5 + m, lambda k: wpt[:, k, at], 2 * CK)):
                    for k in range(CK):
                        T.matmul(ps_x[:, col:col + 1], lhs(k), bfold[:, bias + k:bias + k + 1],
                                 start=(k == 0), stop=(k == CK - 1))
            for k in range(CK):
                last = T.matmul(ps_x[:, 4:5], bq_wide[:, k, :], bfold[:, CK + k:CK + k + 1],
                                start=(k == 0), stop=(k == CK - 1))
            last.then_inc(vec_done, 1)

            pe.wait_ge(gmean_ready, P // GROUP)
            group_means(0)
            group_deviation(0)
            pe.wait_ge(w_ready, 1)
            w0 = places(0, 0)
            for i in range(KPIECES):
                piece(w0[0], 0, i)
            pe.wait_ge(w_ready, 2)
            pe.wait_ge(ident_ready, 1)
            pe.wait_ge(ones_ready, 2)

            all_batches(pe, batch)

            wl = places(B, 0)
            transpose_output(B - 1, -1)
            transpose_maxima(B - 1, 1)
            spread_maxima(B - 1, 1)
            for j in range(QT):
                values(wl[-1], B - 1, j // GT, j % GT, False)
                if j > 0:
                    transpose_output(B - 1, j - 1)
            transpose_output(B - 1, QT - 1)


def kernel(x, L0_conv_norm_w, L0_conv_norm_b, L0_conv_qkv_w, L0_conv_qkv_b, L0_conv_proj_w, L0_conv_proj_b):
    import numpy as np
    import concourse.bacc as bacc
    from concourse import mybir as mb
    from concourse.bass_utils import run_bass_kernel_spmd

    nc = bacc.Bacc("TRN2", target_bir_lowering=False, num_devices=1)
    host = {
        "x": x,
        "norm_w": L0_conv_norm_w,
        "norm_w_cols": np.asarray(L0_conv_norm_w).reshape(2, 128).T,
        "norm_b": L0_conv_norm_b,
        "qkv_w": L0_conv_qkv_w,
        "qkv_b": np.asarray(L0_conv_qkv_b).reshape(6, 128).T,
        "proj_w_t": np.asarray(L0_conv_proj_w).T,
        "proj_b": np.asarray(L0_conv_proj_b).reshape(2, 128).T,
    }
    arrays, args = {}, []
    for name, a in host.items():
        a = np.ascontiguousarray(a)
        arrays[f"in_{name}"] = a
        args.append(nc.dram_tensor(f"in_{name}", a.shape, mb.dt.from_np(a.dtype), kind="ExternalInput").ap())
    args.append(nc.dram_tensor("out_0", x.shape, mb.dt.float32, kind="ExternalOutput").ap())
    attention_program(nc, *args)
    r = run_bass_kernel_spmd(nc, [arrays], core_ids=[0])
    return r.results[0]["out_0"]
```

```python
from contextlib import ExitStack

import concourse.bass as bass
from concourse import mybir


def attention_program(nc, x, norm_w, norm_w_cols, norm_b, qkv_w, qkv_b_cols, proj_w_t, proj_b_cols, out):
    f32, f16 = mybir.dt.float32, mybir.dt.float16
    ALU = mybir.AluOpType
    ACT = mybir.ActivationFunctionType
    AX = mybir.AxisListType

    P = 128
    B, C, HH, WW = x.shape
    N = HH * WW
    CK = C // P
    QT = N // P
    HALF_SLOTS = 2
    HALF = N // 2
    GROUP = C // 8
    EPS = 1e-5
    SCALE = float(C) ** -0.5
    TOP = 4.0
    VEC = 4096.0
    LN_P = 6.931471805599453
    VW = C + 1
    KPIECES = 2 * CK
    PIECES = KPIECES + QT
    GQ = N // HALF_SLOTS
    GT = GQ // P
    BLOCKS = 4
    PAIRS = QT // 2
    BANKS = 4
    XRING = 4

    VALUES_BEFORE = {0: 0, 2: 3, 4: 5, 6: 7}
    VALUES_BEHIND = {0: 1, 1: 2, 3: 4, 5: 6}
    KEYS_BEFORE = {4: 1, 6: 3}
    KEYS_BEHIND = {3: 0, 5: 2}
    EXP, HIGH = 0, 1
    ACT_AT = {3: ((EXP, 0), (HIGH, 0), (EXP, 1)), 4: ((HIGH, 1),), 5: ((EXP, 2), (HIGH, 2)),
              6: ((EXP, 3),), 7: ((HIGH, 3),)}
    LOW_AT = {4: 0, 5: 1, 6: 2, 7: 3}
    ROWSUM_HIGH, ROWSUM_LOW, TOTAL, INVERT, CHUNK0, CHUNK1 = 1, 2, 3, 4, 5, 1

    x_v = x.rearrange("b (c p) h w -> b p c (h w)", p=P)
    out_v = out.rearrange("b (c p) h w -> b p c (h w)", p=P)

    ctx = ExitStack()
    with ctx:
        def sb(name, shape, dt):
            return ctx.enter_context(nc.sbuf_tensor(name, shape, dt))

        def sem(name):
            return ctx.enter_context(nc.semaphore(name))

        ximg = sb("ximg", [P, XRING, CK, N], f32)
        norm32 = sb("norm32", [P, CK, N], f32)
        n_hi = sb("n_hi", [P, 2, CK, N], f16)
        n_lo = sb("n_lo", [P, 2, CK, N], f16)
        t_hi = sb("t_hi", [P, 2, CK, N], f16)
        t_lo = sb("t_lo", [P, 2, CK, N], f16)
        v_hi = sb("v_hi", [P, 2, QT, C], f16)
        v_lo = sb("v_lo", [P, 2, QT, C], f16)
        score = [sb(f"score{h}", [P, QT, GQ], f32) for h in range(2)]
        p_hi = [sb(f"p_hi{h}", [P, QT, GQ], f16) for h in range(2)]
        p_lo = [sb(f"p_lo{h}", [P, QT, GQ], f16) for h in range(2)]
        runmax = [sb(f"runmax{h}", [P, GQ], f32) for h in range(2)]
        maxcol = sb("maxcol", [P, GT], f32)
        maxrow = sb("maxrow", [P, GQ], f32)
        pairsum = sb("pairsum", [P, 2, GQ], f32)
        rowsum = sb("rowsum", [P, GQ], f32)
        rowsum_hi = sb("rowsum_hi", [P, GQ], f16)
        rowsum_lo = sb("rowsum_lo", [P, GQ], f16)
        inverse = sb("inverse", [P, GQ], f32)
        scaled = sb("scaled", [P, CK, GQ], f32)

        wqkv = sb("wqkv", [P, 6, C], f32)
        wnb = sb("wnb", [P, 6, C], f32)
        wpt = sb("wpt", [P, CK, C], f32)
        nw = sb("nw", [P, C], f32)
        nw_cols = sb("nw_cols", [P, 2 * CK + 1], f32)
        m32 = sb("m32", [P, CK, C], f32)
        w32 = sb("w32", [P, CK, C], f32)
        vec32 = sb("vec32", [P, 2 * CK + 1], f32)
        nb_ = sb("nb_", [P, C], f32)
        qkvb = sb("qkvb", [P, 6], f32)
        pb = sb("pb", [P, CK], f32)
        bfold = sb("bfold", [P, 6], f32)
        bq_wide = sb("bq_wide", [P, CK, P], f32)
        m_hi = sb("m_hi", [P, CK, C], f16)
        m_lo = sb("m_lo", [P, CK, C], f16)
        w2_hi = sb("w2_hi", [P, CK, VW], f16)
        w2_lo = sb("w2_lo", [P, CK, VW], f16)
        vecs = sb("vecs", [P, 8], f32)
        bout = sb("bout", [P, CK], f32)
        amax = sb("amax", [P, 3], f32)
        top = sb("top", [P, 2], f32)
        toprec = sb("toprec", [P, 2], f32)
        factor = sb("factor", [P, 2], f32)
        unscale = sb("unscale", [P, 2], f32)
        ident = sb("ident", [P, P], f32)
        ones = sb("ones", [P, P], f32)
        ones16 = sb("ones16", [P, P], f16)
        gmean = sb("gmean", [P, P], f32)
        mhalf = sb("mhalf", [P, CK], f32)

        stats = sb("stats", [P, CK, 2, 6], f32)
        chan = sb("chan", [P, CK, 2], f32)
        grp = sb("grp", [P, CK, 2], f32)
        dev = sb("dev", [P, CK], f32)
        dev2 = sb("dev2", [P, CK], f32)
        var = sb("var", [P, CK], f32)
        rstd = sb("rstd", [P, CK], f32)
        ckey = sb("ckey", [P, QT], f32)
        ln_p = sb("ln_p", [P, 1], f32)

        ps_s = [ctx.enter_context(nc.psum_tensor(f"ps_s{i}", [P, GQ], f32)) for i in range(BANKS)]
        ps_o = [ctx.enter_context(nc.psum_tensor(f"ps_o{i}", [P, 512], f32)) for i in range(2)]
        ps_m = ctx.enter_context(nc.psum_tensor("ps_m", [P, 512], f32))
        ps_x = ctx.enter_context(nc.psum_tensor("ps_x", [P, 512], f32))

        qkv_loaded = sem("qkv_loaded")
        projw_loaded = sem("projw_loaded")
        nb_loaded = sem("nb_loaded")
        small_loaded = sem("small_loaded")
        x_loaded = sem("x_loaded")
        stored = sem("stored")
        consts = sem("consts")
        ident_ready = sem("ident_ready")
        biases_ready = sem("biases_ready")
        m_done = sem("m_done")
        w2_done = sem("w2_done")
        vec_done = sem("vec_done")
        w32_ready = sem("w32_ready")
        scale_ready = sem("scale_ready")
        whi_ready = sem("whi_ready")
        amax_ready = sem("amax_ready")
        top_ready = sem("top_ready")
        w_ready = sem("w_ready")
        dstep = sem("dstep")
        chan_ready = sem("chan_ready")
        gmean_done = sem("gmean_done")
        dev_ready = sem("dev_ready")
        gvar_done = sem("gvar_done")
        var_ready = sem("var_ready")
        rstd_ready = sem("rstd_ready")
        n32_ready = sem("n32_ready")
        nhi_ready = sem("nhi_ready")
        nlo_ready = sem("nlo_ready")
        grp_ready = sem("grp_ready")
        devstep = sem("devstep")
        ones_ready = sem("ones_ready")
        gmean_ready = sem("gmean_ready")
        piece_done = sem("piece_done")
        piece_hi = sem("piece_hi")
        piece_lo = sem("piece_lo")
        c_ready = sem("c_ready")
        scores_done = sem("scores_done")
        copied = sem("copied")
        maxed = sem("maxed")
        maxt_done = sem("maxt_done")
        maxcol_ready = sem("maxcol_ready")
        maxb_done = sem("maxb_done")
        maxrow_ready = sem("maxrow_ready")
        shifted = sem("shifted")
        last_shifted = sem("last_shifted")
        prob_ready = sem("prob_ready")
        phi_ready = sem("phi_ready")
        plo_ready = sem("plo_ready")
        added = sem("added")
        rowsum_ready = sem("rowsum_ready")
        rshi_ready = sem("rshi_ready")
        rslo_ready = sem("rslo_ready")
        total_done = sem("total_done")
        inverse_ready = sem("inverse_ready")
        values_done = sem("values_done")
        scaled_ready = sem("scaled_ready")
        res_ready = sem("res_ready")

        block = ctx.enter_context(nc.Block())

        def count(b, j):
            return b * QT + (j + 1)

        def tile_count(b, h, k):
            return b * (2 * QT) + (h * QT + k + 1)

        def pair_count(b, h, p):
            return b * (2 * PAIRS) + (h * PAIRS + p + 1)

        def group_count(b, h):
            return b * 2 + (h + 1)

        def chunk_count(b, h, c):
            return b * (2 * CK) + (h * CK + c + 1)

        def added_count(b, h, p):
            return b * (2 * (PAIRS - 1)) + (h * (PAIRS - 1) + max(p, 1))

        def before_slot(b, h):
            return (b, 0) if h else (b - 1, 1)

        def piece_count(b, i):
            return b * PIECES + (i + 1)

        class Place:
            def __init__(self, par, ring):
                self.par, self.ring = par, ring

        def places(b, par, eng=None):
            def ring(d):
                if isinstance(b, int):
                    return (b + d) % XRING
                return eng.snap((b + (XRING + d)) & (XRING - 1)) if eng is not None else None
            return {d: Place((par + d) % 2, ring(d)) for d in (-2, -1, 0, 1)}

        def all_batches(eng, batch):
            batch(0, 0, False)
            batch(1, 1, False)
            with eng.Fori(1, B // 2 - 1) as pair:
                for par in range(2):
                    batch(pair * 2 + par, par, False)
            batch(B - 2, 0, False)
            batch(B - 1, 1, True)

        def pieces_at(b, h, k, last, values_at, keys_at):
            if h == 0 and k in values_at:
                return [(0, b, KPIECES + values_at[k])]
            if h == 1 and k in keys_at and not last:
                return [(1, b + 1, keys_at[k])]
            return []

        def pieces_before(b, h, k, last):
            return pieces_at(b, h, k, last, VALUES_BEFORE, KEYS_BEFORE)

        def pieces_behind(b, h, k, last):
            return pieces_at(b, h, k, last, VALUES_BEHIND, KEYS_BEHIND)

        def piece_bank(b, i):
            if not is_batch(b, 0):
                return ps_x
            return (ps_o[0], ps_o[1], ps_m, ps_x)[i] if i < KPIECES else (ps_o[0], ps_o[1], ps_x)[(i - KPIECES) % 3]

        def is_batch(b, n):
            return isinstance(b, int) and b == n

        @block.sync
        def _(sp):
            def load(b, place):
                sp.dma_start(ximg[:, place, :, :], x_v[b]).then_inc(x_loaded, 16)

            def store(b, place, chunks):
                sp.wait_ge(res_ready, chunks)
                sp.dma_start(out_v[b], ximg[:, place, :, :]).then_inc(stored, 16)

            sp.dma_start(wqkv[:, :, :], qkv_w.rearrange("(t p) c -> p t c", p=P)).then_inc(qkv_loaded, 16)
            sp.dma_start(nb_[:, :], norm_b.rearrange("(a c) -> a c", a=1).broadcast_to([P, C])).then_inc(nb_loaded, 16)
            sp.dma_start(wpt[:, :, :], proj_w_t.rearrange("(t p) c -> p t c", p=P)).then_inc(projw_loaded, 16)
            sp.dma_start(qkvb[:, :], qkv_b_cols).then_inc(small_loaded, 16)
            load(0, 0)
            sp.dma_start(nw[:, :], norm_w.rearrange("(a c) -> a c", a=1).broadcast_to([P, C])).then_inc(small_loaded, 16)
            for i in range(2):
                sp.dma_start(nw_cols[:, i * CK:(i + 1) * CK], norm_w_cols).then_inc(small_loaded, 16)
            sp.dma_start(pb[:, :], proj_b_cols).then_inc(small_loaded, 16)
            sp.wait_ge(x_loaded, 16)
            for b in range(1, XRING):
                load(b, b)
                sp.wait_ge(x_loaded, (b + 1) * 16)
            with sp.Fori(0, B - XRING) as b:
                place = sp.snap(b & (XRING - 1))
                chunks = sp.snap((b + 1) * (2 * CK))
                earlier = sp.snap(b * 16 + XRING * 16)
                store_count = sp.snap((b << 4) + 16)
                following = sp.snap(b + XRING)
                store(b, place, chunks)
                sp.wait_ge(stored, store_count)
                sp.wait_ge(x_loaded, earlier)
                load(following, place)
            for b in range(B - XRING, B):
                store(b, b % XRING, (b + 1) * (2 * CK))
                sp.wait_ge(stored, (b + 1) * 16)

        @block.gpsimd
        def _(pool):
            nc.gpsimd.memset(mhalf[:, :], -0.5).then_inc(consts, 1)
            nc.gpsimd.memset(ln_p[:, :], LN_P).then_inc(consts, 1)
            pool.wait_ge(consts, 4)
            nc.gpsimd.affine_select(out=ident[:, :], in_=ones[:, :], compare_op=ALU.is_equal, fill=0.0, base=0,
                                    pattern=[[-1, P]], channel_multiplier=1).then_inc(ident_ready, 1)
            pool.wait_ge(amax_ready, 1)
            nc.gpsimd.partition_all_reduce(top[:, :], amax[:, 0:2], P, bass.bass_isa.ReduceOp.max).then_inc(top_ready, 1)

            def inverse_deviation(b):
                pool.wait_ge(var_ready, b + 1)
                nc.gpsimd.tensor_tensor(rstd[:, :], var[:, :], mhalf[:, :], ALU.pow).then_inc(rstd_ready, 1)

            def split_low(w, b, h):
                pool.wait_ge(nhi_ready, b * 2 + (h + 1))
                at = slice(h * HALF, (h + 1) * HALF)
                nc.gpsimd.tensor_tensor(n_lo[:, w.par, :, at], norm32[:, :, at], n_hi[:, w.par, :, at],
                                        ALU.subtract).then_inc(nlo_ready, 1)

            def take_maximum(b, h, p):
                if p == 0:
                    pool.wait_ge(maxrow_ready, group_count(b, h))
                two = score[h][:, 2 * p:2 * p + 2, :]
                nc.gpsimd.tensor_tensor(two, two, maxrow[:, :].unsqueeze(1).broadcast_to([P, 2, GQ]),
                                        ALU.subtract).then_inc(shifted, 1)

            def add_pairs(b, h):
                for p in range(1, PAIRS):
                    pool.wait_ge(prob_ready, pair_count(b, h, p))
                    if p > 1:
                        pool.wait_ge(added, added_count(b, h, p - 1))
                    first = score[h][:, 0:2, :] if p == 1 else pairsum[:, :, :]
                    nc.gpsimd.tensor_tensor(pairsum[:, :, :], first, score[h][:, 2 * p:2 * p + 2, :],
                                            ALU.add).then_inc(added, 1)

            def fold_sum(b, h):
                pool.wait_ge(added, added_count(b, h, PAIRS - 1))
                nc.gpsimd.tensor_tensor(rowsum[:, :], pairsum[:, 0, :], pairsum[:, 1, :],
                                        ALU.add).then_inc(rowsum_ready, 1)

            def batch(b, par, last):
                w = places(b, par)
                first = is_batch(b, 0)
                if not first:
                    for p in range(PAIRS):
                        take_maximum(b - 1, 1, p)
                    add_pairs(b - 1, 1)
                if not last:
                    inverse_deviation(b + 1)
                if not first:
                    fold_sum(b - 1, 1)
                if not last:
                    split_low(w[1], b + 1, 0)
                take_maximum(b, 0, 0)
                take_maximum(b, 0, 1)
                if not last:
                    split_low(w[1], b + 1, 1)
                take_maximum(b, 0, 2)
                take_maximum(b, 0, 3)
                add_pairs(b, 0)
                fold_sum(b, 0)

            inverse_deviation(0)
            all_batches(pool, batch)
            for p in range(0, PAIRS, 2):
                take_maximum(B - 1, 1, p)

        @block.scalar
        def _(act):
            def split_high(w, b, h):
                act.wait_ge(n32_ready, h + 1 if is_batch(b, 0) else (b + 1) * CK)
                at = slice(h * HALF, (h + 1) * HALF)
                nc.scalar.activation(n_hi[:, w.par, :, at], norm32[:, :, at], ACT.Copy).then_inc(nhi_ready, 1)

            def piece(w, b, i):
                act.wait_ge(piece_done, piece_count(b, i))
                bank = piece_bank(b, i)
                if i < KPIECES:
                    m, h = i % CK, i // CK
                    nc.scalar.activation(t_hi[:, w.par, m, h * HALF:(h + 1) * HALF], bank[:, :],
                                         ACT.Identity, bias=vecs[:, m:m + 1]).then_inc(piece_hi, 1)
                else:
                    nc.scalar.activation(v_hi[:, w.par, i - KPIECES, 0:C], bank[:, 0:C],
                                         ACT.Copy).then_inc(piece_hi, 1)

            def copy_scores(b, h, k):
                act.wait_ge(scores_done, tile_count(b, h, k))
                if h == 0:
                    act.wait_ge(c_ready, count(b, k))
                nc.scalar.activation(score[h][:, k, :], ps_s[k % BANKS][:, :], ACT.Identity,
                                     bias=ckey[:, k:k + 1]).then_inc(copied, 1)

            def copy_maximum(b, h):
                act.wait_ge(maxb_done, group_count(b, h))
                nc.scalar.activation(maxrow[:, :], ps_m[:, :], ACT.Copy).then_inc(maxrow_ready, 1)

            def rowsum_high(b, h):
                act.wait_ge(rowsum_ready, group_count(b, h))
                nc.scalar.activation(rowsum_hi[:, :], rowsum[:, :], ACT.Copy).then_inc(rshi_ready, 1)

            def exponent(b, h, p):
                two = slice(2 * p, 2 * p + 2)
                if is_batch(b, B - 1) and h == 1 and p % 2:
                    act.wait_ge(last_shifted, p // 2 + 1)
                elif is_batch(b, B - 1) and h == 1:
                    act.wait_ge(shifted, pair_count(b, h, p // 2))
                else:
                    act.wait_ge(shifted, pair_count(b, h, p))
                nc.scalar.activation(score[h][:, two, :], score[h][:, two, :], ACT.Exp, bias=ln_p[:, :],
                                     scale=unscale[:, 0:1]).then_inc(prob_ready, 1)

            def probability_high(b, h, p):
                two = slice(2 * p, 2 * p + 2)
                act.wait_ge(prob_ready, pair_count(b, h, p))
                nc.scalar.activation(p_hi[h][:, two, :], score[h][:, two, :], ACT.Copy).then_inc(phi_ready, 1)

            def batch(b, par, last):
                first = is_batch(b, 0)
                w = places(b, par)
                for h in range(2):
                    before = (b, 0) if h else (b - 1, 1)
                    softmax = not (first and h == 0)
                    for k in range(QT):
                        if k == 0 and not first:
                            act.wait_ge(plo_ready, pair_count(b - 1, h, PAIRS - 1))
                        if k in (0, 4, 6) and not first:
                            act.wait_ge(added, added_count(b - 1, h, k // 2))
                        for d, of, i in pieces_before(b, h, k, last):
                            piece(w[d], of, i)
                        copy_scores(b, h, k)
                        for d, of, i in pieces_behind(b, h, k, last):
                            piece(w[d], of, i)
                        if h == 1 and k < 2 and not last:
                            split_high(w[1], b + 1, k)
                        if k == 1 and softmax:
                            copy_maximum(*before)
                        if k == ROWSUM_HIGH and not first:
                            rowsum_high(b - 1, h)
                        if softmax:
                            for kind, pair in ACT_AT.get(k, ()):
                                (exponent, probability_high)[kind](*before, pair)

            act.wait_ge(w2_done, 1)
            act.wait_ge(small_loaded, 5 * 16)
            for k in range(CK):
                nc.scalar.activation(w32[:, k, :], ps_s[1][:, k * C:(k + 1) * C], ACT.Copy,
                                     scale=nw_cols[:, k:k + 1]).then_inc(w32_ready, 1)
            act.wait_ge(scale_ready, 1)
            nc.scalar.activation(m_hi[:, :, :], m32[:, :, :], ACT.Copy, scale=factor[:, 0:1]).then_inc(whi_ready, 1)
            w0 = places(0, 0)
            for h in range(2):
                split_high(w0[0], 0, h)
            nc.scalar.activation(w2_hi[:, :, 0:C], w32[:, :, :], ACT.Copy, scale=factor[:, 1:2]).then_inc(whi_ready, 1)
            act.wait_ge(w_ready, 1)
            for i in range(KPIECES):
                piece(w0[0], 0, i)
            all_batches(act, batch)
            rowsum_high(B - 1, 0)
            copy_maximum(B - 1, 1)
            for p in range(PAIRS):
                exponent(B - 1, 1, p)
                probability_high(B - 1, 1, p)

        @block.vector
        def _(dve):
            steps = [0]

            def step(ins):
                steps[0] += 1
                ins.then_inc(dstep, 1)

            def settle():
                dve.wait_ge(dstep, steps[0])

            V = nc.vector

            def channel_stats(w, b, c):
                if c == 0:
                    dve.wait_ge(x_loaded, (b + 1) * 16)
                for h in range(2):
                    V.bn_stats(stats[:, c, h, :], ximg[:, w.ring, c, h * HALF:(h + 1) * HALF])
                V.drain()
                V.bn_aggr(chan[:, c, :], stats[:, c, :, :].rearrange("p h s -> p (h s)")).then_inc(chan_ready, 1)

            def deviations(b):
                dve.wait_ge(gmean_done, b + 1)
                V.tensor_copy(grp[:, :, :].rearrange("p c s -> p (c s)"), ps_m[:, 0:2 * CK]).then_inc(grp_ready, 1)
                dve.wait_ge(grp_ready, b + 1)
                V.tensor_tensor(dev[:, :], chan[:, :, 0], grp[:, :, 0], ALU.subtract).then_inc(devstep, 1)
                dve.wait_ge(devstep, b + 1)
                V.tensor_tensor(dev2[:, :], dev[:, :], dev[:, :], ALU.mult).then_inc(dev_ready, 1)

            def variance(b):
                dve.wait_ge(gvar_done, b + 1)
                V.scalar_tensor_tensor(out=var[:, :], in0=ps_m[:, 0:CK], scalar=EPS, in1=grp[:, :, 1],
                                       op0=ALU.add, op1=ALU.add).then_inc(var_ready, 1)

            def normalise(w, b):
                dve.wait_ge(rstd_ready, b + 1)
                for c in range(CK):
                    V.tensor_scalar(norm32[:, c, :], ximg[:, w.ring, c, :], grp[:, c, 0:1],
                                    rstd[:, c:c + 1], ALU.subtract, ALU.mult).then_inc(n32_ready, 1)

            def piece(w, b, i):
                dve.wait_ge(piece_hi, piece_count(b, i))
                bank = piece_bank(b, i)
                if i < KPIECES:
                    m, h = i % CK, i // CK
                    at = slice(h * HALF, (h + 1) * HALF)
                    V.scalar_tensor_tensor(out=t_lo[:, w.par, m, at], in0=bank[:, :], scalar=vecs[:, m:m + 1],
                                           in1=t_hi[:, w.par, m, at], op0=ALU.add, op1=ALU.subtract).then_inc(piece_lo, 1)
                else:
                    k = i - KPIECES
                    V.tensor_scalar(ckey[:, k:k + 1], bank[:, C:VW], vecs[:, 4:5], None, ALU.add).then_inc(c_ready, 1)
                    V.tensor_tensor(v_lo[:, w.par, k, 0:C], bank[:, 0:C], v_hi[:, w.par, k, 0:C],
                                    ALU.subtract).then_inc(piece_lo, 1)

            def maximum(b, h, k):
                dve.wait_ge(copied, tile_count(b, h, k))
                if k == 0:
                    V.tensor_scalar(runmax[h][:, :], ps_s[0][:, :], ckey[:, 0:1], None, ALU.add).then_inc(maxed, 1)
                else:
                    dve.wait_ge(maxed, tile_count(b, h, k - 1))
                    V.scalar_tensor_tensor(out=runmax[h][:, :], in0=ps_s[k % BANKS][:, :], scalar=ckey[:, k:k + 1],
                                           in1=runmax[h][:, :], op0=ALU.add, op1=ALU.max).then_inc(maxed, 1)

            def reduce_maxima(b, h):
                dve.wait_ge(maxt_done, group_count(b, h))
                V.tensor_reduce(maxcol[:, :], ps_m[:, :].rearrange("p (t k) -> p t k", t=GT), AX.X, ALU.max) \
                    .then_inc(maxcol_ready, 1)

            def prob_low(b, h, p):
                two = slice(2 * p, 2 * p + 2)
                dve.wait_ge(phi_ready, pair_count(b, h, p))
                V.tensor_tensor(p_lo[h][:, two, :], score[h][:, two, :], p_hi[h][:, two, :],
                                ALU.subtract).then_inc(plo_ready, 1)

            def rowsum_low(b, h):
                dve.wait_ge(rshi_ready, group_count(b, h))
                V.tensor_tensor(rowsum_lo[:, :], rowsum[:, :], rowsum_hi[:, :], ALU.subtract).then_inc(rslo_ready, 1)

            def invert(b, h, bank):
                dve.wait_ge(total_done, group_count(b, h))
                V.reciprocal(inverse[:, :], bank[:, :]).then_inc(inverse_ready, 1)

            def result(w, b, h, c, bank):
                dve.wait_ge(values_done, chunk_count(b, h, c))
                dve.wait_ge(inverse_ready, group_count(b, h))
                V.scalar_tensor_tensor(out=scaled[:, c, :], in0=bank[:, :], scalar=unscale[:, 1:2],
                                       in1=inverse[:, :], op0=ALU.mult, op1=ALU.mult).then_inc(scaled_ready, 1)
                at = slice(h * GQ, (h + 1) * GQ)
                dve.wait_ge(scaled_ready, chunk_count(b, h, c))
                V.scalar_tensor_tensor(out=ximg[:, w.ring, c, at], in0=scaled[:, c, :],
                                       scalar=bout[:, c:c + 1], in1=ximg[:, w.ring, c, at],
                                       op0=ALU.add, op1=ALU.add).then_inc(res_ready, 1)

            def batch(b, par, last):
                first, second = is_batch(b, 0), is_batch(b, 1)
                w = places(b, par, dve)
                for h in range(2):
                    before = (b, 0) if h else (b - 1, 1)
                    softmax = not (first and h == 0)
                    for k in range(QT):
                        if k == ROWSUM_LOW and not first:
                            rowsum_low(b - 1, h)
                        if k == INVERT and not first:
                            invert(b - 1, h, ps_o[1])
                        for d, of, i in pieces_before(b, h, k, last):
                            piece(w[d], of, i)
                        if k == 0 and softmax:
                            reduce_maxima(*before)
                        maximum(b, h, k)
                        for d, of, i in pieces_behind(b, h, k, last):
                            piece(w[d], of, i)
                        if k == CHUNK1 and not first and not (second and h == 0):
                            result(w[-1] if h else w[-2], *before_slot(b - 1, h), 1, ps_o[1])
                        if k == CHUNK0 and not first:
                            result(w[-1], b - 1, h, 0, ps_o[0])
                        if not last:
                            if h == 0 and k in (0, 2):
                                channel_stats(w[1], b + 1, k // 2)
                            if h == 0 and k == 5:
                                deviations(b + 1)
                            if h == 0 and k == 7:
                                variance(b + 1)
                            if h == 1 and k == 0:
                                normalise(w[1], b + 1)
                        if k in LOW_AT and softmax:
                            prob_low(*before, LOW_AT[k])

            V.memset(gmean[:, :], 0.0).then_inc(consts, 1)
            V.memset(ones[:, :], 1.0).then_inc(consts, 1)
            dve.wait_ge(consts, 4)
            for g in range(P // GROUP):
                at = slice(g * GROUP, (g + 1) * GROUP)
                V.memset(gmean[at, at], 1.0 / GROUP).then_inc(gmean_ready, 1)

            V.memset(ones16[:, :], 1.0).then_inc(ones_ready, 1)
            step(V.memset(nw_cols[:, 2 * CK:], 1.0))

            dve.wait_ge(qkv_loaded, 16)
            dve.wait_ge(nb_loaded, 16)
            step(V.tensor_tensor(wnb[:, :, :], wqkv[:, :, :], nb_[:, :].unsqueeze(1).broadcast_to([P, 6, C]), ALU.mult))
            settle()
            step(V.tensor_reduce(bfold[:, :], wnb[:, :, :], AX.X, ALU.add))
            settle()
            dve.wait_ge(small_loaded, 5 * 16)
            step(V.tensor_tensor(bfold[:, :], bfold[:, :], qkvb[:, :], ALU.add))
            settle()
            for k in range(CK):
                V.tensor_scalar(bq_wide[:, k, :], ones[:, :], bfold[:, k:k + 1], None, ALU.mult) \
                    .then_inc(biases_ready, 1)

            w0 = places(0, 0)
            for c in range(CK):
                channel_stats(w0[0], 0, c)

            dve.wait_ge(m_done, 1)
            for k in range(CK):
                step(V.scalar_tensor_tensor(out=m32[:, k, :], in0=ps_s[0][:, k * C:(k + 1) * C],
                                            scalar=nw_cols[:, k:k + 1], in1=nw[:, :], op0=ALU.mult, op1=ALU.mult))
            dve.wait_ge(vec_done, 1)
            step(V.tensor_tensor(vec32[:, :], ps_x[:, 0:2 * CK + 1], nw_cols[:, :], ALU.mult))
            step(V.tensor_tensor(bout[:, :], ps_x[:, 5:5 + CK], pb[:, :], ALU.add))
            deviations(0)
            settle()
            step(V.tensor_reduce(amax[:, 0:1], m32[:, :, :].rearrange("p k c -> p (k c)"), AX.X, ALU.max,
                                 apply_absolute_value=True))
            step(V.tensor_reduce(amax[:, 2:3], vec32[:, 0:2 * CK], AX.X, ALU.max, apply_absolute_value=True))
            variance(0)
            dve.wait_ge(w32_ready, CK)
            step(V.tensor_reduce(amax[:, 1:2], w32[:, :, :].rearrange("p k c -> p (k c)"), AX.X, ALU.max,
                                 apply_absolute_value=True))
            settle()
            V.scalar_tensor_tensor(out=amax[:, 0:1], in0=amax[:, 2:3], scalar=1.0 / VEC, in1=amax[:, 0:1],
                                   op0=ALU.mult, op1=ALU.max).then_inc(amax_ready, 1)

            dve.wait_ge(rstd_ready, 1)
            for h in range(2):
                at = slice(h * HALF, (h + 1) * HALF)
                for c in range(CK):
                    last = V.tensor_scalar(norm32[:, c, at], ximg[:, 0, c, at], grp[:, c, 0:1],
                                           rstd[:, c:c + 1], ALU.subtract, ALU.mult)
                last.then_inc(n32_ready, 1)

            dve.wait_ge(top_ready, 1)
            step(V.tensor_scalar(top[:, :], top[:, :], 1e-30, None, ALU.max))
            settle()
            step(V.reciprocal(toprec[:, :], top[:, :]))
            step(V.tensor_scalar(unscale[:, 0:1], top[:, 0:1], SCALE / TOP, None, ALU.mult))
            step(V.tensor_scalar(unscale[:, 1:2], top[:, 1:2], 1.0 / TOP, None, ALU.mult))
            settle()
            V.tensor_scalar(factor[:, :], toprec[:, :], TOP, None, ALU.mult).then_inc(scale_ready, 1)
            dve.wait_ge(scale_ready, 1)
            step(V.tensor_scalar(vecs[:, 0:5], vec32[:, :], factor[:, 0:1], None, ALU.mult))

            dve.wait_ge(whi_ready, 1)
            V.scalar_tensor_tensor(out=m_lo[:, :, :].rearrange("p k c -> p (k c)"),
                                   in0=m32[:, :, :].rearrange("p k c -> p (k c)"), scalar=factor[:, 0:1],
                                   in1=m_hi[:, :, :].rearrange("p k c -> p (k c)"),
                                   op0=ALU.mult, op1=ALU.subtract).then_inc(w_ready, 1)
            for h in range(2):
                at = slice(h * HALF, (h + 1) * HALF)
                dve.wait_ge(nhi_ready, h + 1)
                V.tensor_tensor(n_lo[:, 0, :, at], norm32[:, :, at], n_hi[:, 0, :, at], ALU.subtract) \
                    .then_inc(nlo_ready, 1)

            settle()
            c_cols = vecs[:, CK:2 * CK].unsqueeze(2)
            step(V.tensor_copy(w2_hi[:, :, C:VW], c_cols))
            dve.wait_ge(whi_ready, 2)
            V.scalar_tensor_tensor(out=w2_lo[:, :, 0:C], in0=w32[:, :, :], scalar=factor[:, 1:2],
                                   in1=w2_hi[:, :, 0:C], op0=ALU.mult, op1=ALU.subtract)
            settle()
            V.tensor_tensor(w2_lo[:, :, C:VW], c_cols, w2_hi[:, :, C:VW], ALU.subtract).then_inc(w_ready, 1)

            for i in range(KPIECES):
                piece(w0[0], 0, i)

            all_batches(dve, batch)

            wl = places(B, 0)
            result(wl[-2], B - 2, 1, 1, ps_o[1])
            reduce_maxima(B - 1, 1)
            rowsum_low(B - 1, 0)
            dve.wait_ge(maxrow_ready, group_count(B - 1, 1))
            for p in range(1, PAIRS, 2):
                two = score[1][:, 2 * p:2 * p + 2, :]
                V.tensor_tensor(two, two, maxrow[:, :].unsqueeze(1).broadcast_to([P, 2, GQ]),
                                ALU.subtract).then_inc(last_shifted, 1)
            invert(B - 1, 0, ps_o[1])
            prob_low(B - 1, 1, 0)
            result(wl[-1], B - 1, 0, 0, ps_o[0])
            prob_low(B - 1, 1, 1)
            result(wl[-1], B - 1, 0, 1, ps_o[1])
            prob_low(B - 1, 1, 2)
            prob_low(B - 1, 1, 3)
            invert(B - 1, 1, ps_s[2])
            for c in range(CK):
                result(wl[-1], B - 1, 1, c, ps_s[c])

        @block.tensor
        def _(pe):
            T = nc.tensor

            def split_product(dst, ah, al, bh, bl, chunks):
                n = 0
                for k in range(chunks):
                    for lhs, rhs in ((ah, bh), (ah, bl), (al, bh)):
                        n += 1
                        last = T.matmul(dst, lhs(k), rhs(k), start=(n == 1), stop=(n == 3 * chunks))
                return last

            def group_means(b):
                pe.wait_ge(chan_ready, (b + 1) * CK)
                T.matmul(ps_m[:, 0:2 * CK], gmean[:, :], chan[:, :, :].rearrange("p c s -> p (c s)"),
                         start=True, stop=True).then_inc(gmean_done, 1)

            def group_deviation(b):
                pe.wait_ge(dev_ready, b + 1)
                T.matmul(ps_m[:, 0:CK], gmean[:, :], dev2[:, :], start=True, stop=True).then_inc(gvar_done, 1)

            def piece(w, b, i):
                if is_batch(b, 0) and i < KPIECES:
                    pass
                elif is_batch(b, 0):
                    pe.wait_ge(piece_lo, piece_count(b, i - 4 if i < KPIECES + 2 else i - 3))
                elif i > 0:
                    pe.wait_ge(piece_lo, piece_count(b, i - 1))
                else:
                    pe.wait_ge(piece_lo, piece_count(b - 1, PIECES - 1))
                bank = piece_bank(b, i)
                if i < KPIECES:
                    m, h = i % CK, i // CK
                    pe.wait_ge(nlo_ready, b * 2 + (h + 1))
                    at = slice(h * HALF, (h + 1) * HALF)
                    split_product(bank[:, :],
                                  lambda k: m_hi[:, k, m * P:(m + 1) * P], lambda k: m_lo[:, k, m * P:(m + 1) * P],
                                  lambda k: n_hi[:, w.par, k, at], lambda k: n_lo[:, w.par, k, at], CK).then_inc(piece_done, 1)
                else:
                    at = slice((i - KPIECES) * P, (i - KPIECES + 1) * P)
                    split_product(bank[:, 0:VW],
                                  lambda k: n_hi[:, w.par, k, at], lambda k: n_lo[:, w.par, k, at],
                                  lambda k: w2_hi[:, k, :], lambda k: w2_lo[:, k, :], CK).then_inc(piece_done, 1)

            def scores(w, b, h, k, fresh):
                if not (fresh and k < BANKS):
                    pe.wait_ge(maxed, tile_count(b, h, k - BANKS))
                at = slice(k * P, (k + 1) * P)
                queries = slice(h * GQ, (h + 1) * GQ)
                split_product(ps_s[k % BANKS][:, :],
                              lambda c: t_hi[:, w.par, c, at], lambda c: t_lo[:, w.par, c, at],
                              lambda c: n_hi[:, w.par, c, queries], lambda c: n_lo[:, w.par, c, queries],
                              CK).then_inc(scores_done, 1)

            def transpose_maxima(b, h):
                pe.wait_ge(maxed, tile_count(b, h, QT - 1))
                for t in range(GT):
                    last = T.transpose(ps_m[:, t * P:(t + 1) * P], runmax[h][:, t * P:(t + 1) * P], ident[:, :])
                last.then_inc(maxt_done, 1)

            def spread_maxima(b, h):
                pe.wait_ge(maxcol_ready, group_count(b, h))
                for t in range(GT):
                    last = T.transpose(ps_m[:, t * P:(t + 1) * P], maxcol[:, t:t + 1].broadcast_to([P, P]), ident[:, :])
                last.then_inc(maxb_done, 1)

            def values_of_tile(dst, w, h, c, k, first, end):
                vh, vl = (v[:, w.par, k, c * P:(c + 1) * P] for v in (v_hi, v_lo))
                T.matmul(dst, vh, p_hi[h][:, k, :], start=first, stop=False)
                T.matmul(dst, vh, p_lo[h][:, k, :], start=False, stop=False)
                return T.matmul(dst, vl, p_hi[h][:, k, :], start=False, stop=end)

            def values(w, b, h, i):
                c, half = i // 2, i % 2
                if i == 0:
                    pe.wait_ge(plo_ready, pair_count(b, h, PAIRS - 1))
                if i == 0 and not (is_batch(b, 0) and h == 0):
                    pe.wait_ge(scaled_ready, chunk_count(b, h, c) - CK)
                if i == 2:
                    pe.wait_ge(inverse_ready, group_count(b, h))
                for k in range(half * QT // 2, (half + 1) * QT // 2):
                    last = values_of_tile(ps_o[c][:, :], w, h, c, k, k == 0, k == QT - 1)
                if half:
                    last.then_inc(values_done, 1)

            def total(b, h):
                pe.wait_ge(rslo_ready, group_count(b, h))
                if not (is_batch(b, 0) and h == 0):
                    pe.wait_ge(scaled_ready, chunk_count(b, h, 1) - CK)
                T.matmul(ps_o[1][:, :], ones16[:, :], rowsum_hi[:, :], start=True, stop=False)
                T.matmul(ps_o[1][:, :], ones16[:, :], rowsum_lo[:, :], start=False, stop=True).then_inc(total_done, 1)

            def batch(b, par, last):
                first = is_batch(b, 0)
                w = places(b, par)
                for h in range(2):
                    before = (b, 0) if h else (b - 1, 1)
                    softmax = not (first and h == 0)
                    for k in range(QT):
                        for d, of, i in pieces_before(b, h, k, last):
                            piece(w[d], of, i)
                        if first and h == 0 and k == 0:
                            pe.wait_ge(piece_lo, KPIECES)
                        scores(w[0], b, h, k, first and h == 0)
                        if k == 0 and softmax:
                            if h == 1 and not last:
                                pe.wait_ge(var_ready, b + 2)
                            transpose_maxima(*before)
                        for d, of, i in pieces_behind(b, h, k, last):
                            piece(w[d], of, i)
                        if h == 0 and k == 4 and not last:
                            if not first:
                                pe.wait_ge(maxrow_ready, group_count(b - 1, 1))
                            group_means(b + 1)
                        if h == 0 and k == 6 and not last:
                            group_deviation(b + 1)
                        if k == 1 and softmax:
                            spread_maxima(*before)
                        if k % 2 == 1 and not first:
                            if k == TOTAL:
                                total(b - 1, h)
                            values(w[-1], b - 1, h, k // 2)

            pe.wait_ge(qkv_loaded, 16)
            for bank, first, rhs, done in ((ps_s[0], CK, wqkv, m_done), (ps_s[1], 2 * CK, wpt, w2_done)):
                if rhs is wpt:
                    pe.wait_ge(projw_loaded, 16)
                for m in range(CK):
                    for k in range(CK):
                        last = T.matmul(bank[:, m * C:(m + 1) * C], wqkv[:, first + k, m * P:(m + 1) * P],
                                        rhs[:, k, :], start=(k == 0), stop=(k == CK - 1))
                last.then_inc(done, 1)
            pe.wait_ge(biases_ready, CK)
            for m in range(CK):
                at = slice(m * P, (m + 1) * P)
                for col, lhs, bias in ((m, lambda k: wqkv[:, k, at], CK),
                                       (CK + m, lambda k: wqkv[:, CK + k, at], 0),
                                       (5 + m, lambda k: wpt[:, k, at], 2 * CK)):
                    for k in range(CK):
                        T.matmul(ps_x[:, col:col + 1], lhs(k), bfold[:, bias + k:bias + k + 1],
                                 start=(k == 0), stop=(k == CK - 1))
            for k in range(CK):
                last = T.matmul(ps_x[:, 4:5], bq_wide[:, k, :], bfold[:, CK + k:CK + k + 1],
                                start=(k == 0), stop=(k == CK - 1))
            last.then_inc(vec_done, 1)

            pe.wait_ge(gmean_ready, P // GROUP)
            group_means(0)
            group_deviation(0)
            pe.wait_ge(w_ready, 1)
            w0 = places(0, 0)
            for i in range(KPIECES):
                piece(w0[0], 0, i)
            pe.wait_ge(w_ready, 2)
            pe.wait_ge(ident_ready, 1)
            pe.wait_ge(ones_ready, 1)

            all_batches(pe, batch)

            wl = places(B, 0)
            transpose_maxima(B - 1, 1)
            values(wl[-1], B - 1, 0, 0)
            spread_maxima(B - 1, 1)
            values(wl[-1], B - 1, 0, 1)
            total(B - 1, 0)
            values(wl[-1], B - 1, 0, 2)
            values(wl[-1], B - 1, 0, 3)
            for p in range(PAIRS):
                pe.wait_ge(plo_ready, pair_count(B - 1, 1, p))
                for k in (2 * p, 2 * p + 1):
                    T.matmul(ps_s[2][:, :], ones16[:, :], p_hi[1][:, k, :], start=(k == 0), stop=False)
                    last = T.matmul(ps_s[2][:, :], ones16[:, :], p_lo[1][:, k, :], start=False, stop=(k == QT - 1))
                if p == PAIRS - 1:
                    last.then_inc(total_done, 1)
                for c in range(CK):
                    for k in (2 * p, 2 * p + 1):
                        last = values_of_tile(ps_s[c][:, :], wl[-1], 1, c, k, k == 0, k == QT - 1)
                    if p == PAIRS - 1:
                        last.then_inc(values_done, 1)


def kernel(x, L0_conv_norm_w, L0_conv_norm_b, L0_conv_qkv_w, L0_conv_qkv_b, L0_conv_proj_w, L0_conv_proj_b):
    import numpy as np
    import concourse.bacc as bacc
    from concourse import mybir as mb
    from concourse.bass_utils import run_bass_kernel_spmd

    nc = bacc.Bacc("TRN2", target_bir_lowering=False, num_devices=1)
    host = {
        "x": x,
        "norm_w": L0_conv_norm_w,
        "norm_w_cols": np.asarray(L0_conv_norm_w).reshape(2, 128).T,
        "norm_b": L0_conv_norm_b,
        "qkv_w": L0_conv_qkv_w,
        "qkv_b": np.asarray(L0_conv_qkv_b).reshape(6, 128).T,
        "proj_w_t": np.asarray(L0_conv_proj_w).T,
        "proj_b": np.asarray(L0_conv_proj_b).reshape(2, 128).T,
    }
    arrays, args = {}, []
    for name, a in host.items():
        a = np.ascontiguousarray(a)
        arrays[f"in_{name}"] = a
        args.append(nc.dram_tensor(f"in_{name}", a.shape, mb.dt.from_np(a.dtype), kind="ExternalInput").ap())
    args.append(nc.dram_tensor("out_0", x.shape, mb.dt.float32, kind="ExternalOutput").ap())
    attention_program(nc, *args)
    r = run_bass_kernel_spmd(nc, [arrays], core_ids=[0])
    return r.results[0]["out_0"]
```
